# Optimizing a Trainium2 kernel written in Bass

```python
import numpy as np
import jax
import jax.numpy as jnp

def _softmax(x, axis=-1):
    return jax.nn.softmax(x, axis=axis)

def _gelu(x):
    return jax.nn.gelu(x, approximate=True)

def _silu(x):
    return jax.nn.silu(x)

def _sigmoid(x):
    return jax.nn.sigmoid(x)

def _layernorm(x, axis=-1, eps=1e-05):
    m = jnp.mean(x, axis=axis, keepdims=True)
    v = jnp.var(x, axis=axis, keepdims=True)
    return (x - m) / jnp.sqrt(v + eps)

def _scatter_add(tgt, idx, src, axis=0):
    return tgt.at[idx].add(src)

def _segment_sum(src, seg, n):
    return jax.ops.segment_sum(src, seg, n)
kernel_name = 'mk_seq_postln_d1_jaxref_r4_2cc779'

def setup_inputs(seed: int=0):
    np.random.seed(seed)
    _w = jnp.asarray

    def _L0_attn_setup():
        import jax, jax.numpy as jnp
        import numpy as np
        D_MODEL = 256
        D_STATE = 16
        D_CONV = 4
        D_INNER = 2 * D_MODEL
        DT_RANK = (D_MODEL + 15) // 16
        BATCH, SEQLEN = (2, 256)

        def _forward(hidden_states, in_proj_w, conv_w, conv_b, x_proj_w, dt_proj_w, dt_proj_b, A_log, D, out_proj_w):
            B, L, _ = hidden_states.shape
            xz = hidden_states @ in_proj_w.T
            x, z = jnp.split(xz, 2, axis=-1)
            xc = jnp.transpose(x, (0, 2, 1))
            xc = jax.lax.conv_general_dilated(xc, conv_w, window_strides=(1,), padding=[(D_CONV - 1, 0)], feature_group_count=D_INNER, dimension_numbers=('NCH', 'OIH', 'NCH')) + conv_b[None, :, None]
            xc = jax.nn.silu(xc)
            u = jnp.transpose(xc, (0, 2, 1)).astype(jnp.float32)
            x_dbl = u @ x_proj_w.T
            dt_low, Bp, Cp = jnp.split(x_dbl, [DT_RANK, DT_RANK + D_STATE], axis=-1)
            dt = dt_low @ dt_proj_w.T + dt_proj_b
            delta = jax.nn.softplus(dt + dt_proj_b)
            A = -jnp.exp(A_log.astype(jnp.float32))
            dA = jnp.exp(jnp.einsum('bld,dn->lbdn', delta, A))
            dBu = jnp.einsum('bld,bln,bld->lbdn', delta, Bp.astype(jnp.float32), u)
            C_t = jnp.transpose(Cp.astype(jnp.float32), (1, 0, 2))

            def step(state, inp):
                a, b, c = inp
                state = a * state + b
                y = jnp.einsum('bdn,bn->bd', state, c)
                return (state, y)
            x0 = jnp.zeros((B, D_INNER, D_STATE), jnp.float32)
            _, ys = jax.lax.scan(step, x0, (dA, dBu, C_t))
            y = jnp.transpose(ys, (1, 0, 2))
            y = y + u * D.astype(jnp.float32)
            y = y * jax.nn.silu(z.astype(jnp.float32))
            y = y.astype(hidden_states.dtype)
            return y @ out_proj_w.T
        key = jax.random.key(seed)
        ks = jax.random.split(key, 8)
        s = lambda k, shape, scale=0.02: jax.random.normal(k, shape, jnp.float32) * scale
        return {'hidden_states': jax.random.normal(ks[0], (BATCH, SEQLEN, D_MODEL), jnp.float32), 'in_proj_w': s(ks[1], (2 * D_INNER, D_MODEL)), 'conv_w': s(ks[2], (D_INNER, 1, D_CONV), 0.3), 'conv_b': jnp.zeros((D_INNER,), jnp.float32), 'x_proj_w': s(ks[3], (DT_RANK + 2 * D_STATE, D_INNER)), 'dt_proj_w': s(ks[4], (D_INNER, DT_RANK), 0.1), 'dt_proj_b': jax.random.uniform(ks[5], (D_INNER,), jnp.float32, minval=-5.0, maxval=-2.0), 'A_log': jnp.log(jnp.broadcast_to(jnp.arange(1, D_STATE + 1, dtype=jnp.float32), (D_INNER, D_STATE))), 'D': jnp.ones((D_INNER,), jnp.float32), 'out_proj_w': s(ks[6], (D_MODEL, D_INNER))}
    _L0_attn_in = _L0_attn_setup()

    def _L0_ffn_setup():
        import jax, jax.numpy as jnp
        import numpy as np
        B, S, D = (4, 512, 256)
        N_EXPERTS, EXPERT_SIZE = (16, 64)
        WIDTH = N_EXPERTS * EXPERT_SIZE
        key = jax.random.key(seed)
        k_x, k_w1, k_w2, k_g = jax.random.split(key, 4)
        x = jax.random.normal(k_x, (B, S, D), dtype=jnp.float32)
        w1 = jax.random.normal(k_w1, (D, WIDTH), dtype=jnp.float32) / np.sqrt(D).astype(np.float32)
        b1 = jnp.zeros((WIDTH,), dtype=jnp.float32)
        w2 = jax.random.normal(k_w2, (WIDTH, D), dtype=jnp.float32) / np.sqrt(WIDTH).astype(np.float32)
        b2 = jnp.zeros((D,), dtype=jnp.float32)
        return {'x': x, 'w1': w1, 'b1': b1, 'w2': w2, 'b2': b2}
    _L0_ffn_in = _L0_ffn_setup()
    _d = {'L0_attn_hidden_states': _L0_attn_in['hidden_states'], 'L0_attn_in_proj_w': _L0_attn_in['in_proj_w'], 'L0_attn_conv_w': _L0_attn_in['conv_w'], 'L0_attn_conv_b': _L0_attn_in['conv_b'], 'L0_attn_x_proj_w': _L0_attn_in['x_proj_w'], 'L0_attn_dt_proj_w': _L0_attn_in['dt_proj_w'], 'L0_attn_dt_proj_b': _L0_attn_in['dt_proj_b'], 'L0_attn_A_log': _L0_attn_in['A_log'], 'L0_attn_D': _L0_attn_in['D'], 'L0_attn_out_proj_w': _L0_attn_in['out_proj_w'], 'L0_ffn_w1': _L0_ffn_in['w1'], 'L0_ffn_b1': _L0_ffn_in['b1'], 'L0_ffn_w2': _L0_ffn_in['w2'], 'L0_ffn_b2': _L0_ffn_in['b2']}
    _x0 = _d['L0_attn_hidden_states']
    _d['L0_attn_hidden_states'] = jax.random.normal(jax.random.fold_in(jax.random.key(seed), 1), (4, 1024, 256), dtype=_x0.dtype)
    del _x0
    return _d

def reference(L0_attn_hidden_states, L0_attn_in_proj_w, L0_attn_conv_w, L0_attn_conv_b, L0_attn_x_proj_w, L0_attn_dt_proj_w, L0_attn_dt_proj_b, L0_attn_A_log, L0_attn_D, L0_attn_out_proj_w, L0_ffn_w1, L0_ffn_b1, L0_ffn_w2, L0_ffn_b2):

    def _L0_attn_ref(hidden_states, in_proj_w, conv_w, conv_b, x_proj_w, dt_proj_w, dt_proj_b, A_log, D, out_proj_w):
        import jax, jax.numpy as jnp
        import numpy as np
        D_MODEL = 256
        D_STATE = 16
        D_CONV = 4
        D_INNER = 2 * D_MODEL
        DT_RANK = (D_MODEL + 15) // 16
        BATCH, SEQLEN = (2, 256)

        def _forward(hidden_states, in_proj_w, conv_w, conv_b, x_proj_w, dt_proj_w, dt_proj_b, A_log, D, out_proj_w):
            B, L, _ = hidden_states.shape
            xz = hidden_states @ in_proj_w.T
            x, z = jnp.split(xz, 2, axis=-1)
            xc = jnp.transpose(x, (0, 2, 1))
            xc = jax.lax.conv_general_dilated(xc, conv_w, window_strides=(1,), padding=[(D_CONV - 1, 0)], feature_group_count=D_INNER, dimension_numbers=('NCH', 'OIH', 'NCH')) + conv_b[None, :, None]
            xc = jax.nn.silu(xc)
            u = jnp.transpose(xc, (0, 2, 1)).astype(jnp.float32)
            x_dbl = u @ x_proj_w.T
            dt_low, Bp, Cp = jnp.split(x_dbl, [DT_RANK, DT_RANK + D_STATE], axis=-1)
            dt = dt_low @ dt_proj_w.T + dt_proj_b
            delta = jax.nn.softplus(dt + dt_proj_b)
            A = -jnp.exp(A_log.astype(jnp.float32))
            dA = jnp.exp(jnp.einsum('bld,dn->lbdn', delta, A))
            dBu = jnp.einsum('bld,bln,bld->lbdn', delta, Bp.astype(jnp.float32), u)
            C_t = jnp.transpose(Cp.astype(jnp.float32), (1, 0, 2))

            def step(state, inp):
                a, b, c = inp
                state = a * state + b
                y = jnp.einsum('bdn,bn->bd', state, c)
                return (state, y)
            x0 = jnp.zeros((B, D_INNER, D_STATE), jnp.float32)
            _, ys = jax.lax.scan(step, x0, (dA, dBu, C_t))
            y = jnp.transpose(ys, (1, 0, 2))
            y = y + u * D.astype(jnp.float32)
            y = y * jax.nn.silu(z.astype(jnp.float32))
            y = y.astype(hidden_states.dtype)
            return y @ out_proj_w.T
        return _forward(hidden_states, in_proj_w, conv_w, conv_b, x_proj_w, dt_proj_w, dt_proj_b, A_log, D, out_proj_w)

    def _L0_ffn_ref(x, w1, b1, w2, b2):
        import jax, jax.numpy as jnp
        import numpy as np
        B, S, D = (4, 512, 256)
        N_EXPERTS, EXPERT_SIZE = (16, 64)
        WIDTH = N_EXPERTS * EXPERT_SIZE
        h = jax.nn.relu(jnp.einsum('bsd,dw->bsw', x, w1) + b1)
        return jnp.einsum('bsw,wd->bsd', h, w2) + b2
    x = L0_attn_hidden_states
    x = _layernorm(x + _L0_attn_ref(x, L0_attn_in_proj_w, L0_attn_conv_w, L0_attn_conv_b, L0_attn_x_proj_w, L0_attn_dt_proj_w, L0_attn_dt_proj_b, L0_attn_A_log, L0_attn_D, L0_attn_out_proj_w), axis=-1)
    x = _layernorm(x + _L0_ffn_ref(x, L0_ffn_w1, L0_ffn_b1, L0_ffn_w2, L0_ffn_b2), axis=-1)
    return x

_drawn_inputs = setup_inputs


def setup_inputs(seed=0):
    import zlib

    import numpy as np

    out = dict(_drawn_inputs(seed))
    spreads = {'L0_attn_conv_b': (0.0, 0.8),
     'L0_attn_D': (1.0, 0.6),
     'L0_ffn_b1': (0.0, 0.1),
     'L0_ffn_b2': (0.0, 0.1)}
    factors = {'L0_attn_in_proj_w': 6.111,
     'L0_attn_conv_w': 6.415,
     'L0_attn_x_proj_w': 8.0,
     'L0_attn_dt_proj_w': 8.0,
     'L0_attn_dt_proj_b': 8.0,
     'L0_attn_A_log': 8.0,
     'L0_attn_out_proj_w': 5.717}
    for name, (base, spread) in spreads.items():
        noise = np.random.default_rng([zlib.crc32(name.encode()), seed]).standard_normal(out[name].shape)
        drawn = base * np.exp(spread * noise) if base else spread * noise
        out[name] = jnp.asarray(drawn.astype(out[name].dtype))
    for name, factor in factors.items():
        out[name] = (out[name] * factor).astype(out[name].dtype)
    return out
```

```python
import numpy as np
import concourse.bass as bass
from concourse import mybir
from contextlib import ExitStack

F32 = mybir.dt.float32
ALU = mybir.AluOpType
ACT = mybir.ActivationFunctionType

P = 128
BATCH, SEQ, DM = 4, 1024, 256
DI, NS, RK, TAPS = 512, 16, 16, 4
FW = 1024
L = 512
UNITS = BATCH * SEQ // L
KT = DI // P
MT = DM // P
LT = L // P
WT = FW // P
XR = RK + 2 * NS
PW = 2 * P
QS = NS * KT
EPS = 1e-5
HALO = TAPS - 1
B_RING, DB_RING, H_RING = 4, 4, 3

SHARED = (1, 4, 8, 11)
OWN = tuple(n for n in range(NS) if n not in SHARED)
T_RING = 3

X_PE, X_ACT, X_DVE, X_TANH, U_DVE = (0, 6, 12, 16), (3, 10, 15, 20), (5, 12, 17, 22), (9, 14, 20, 25), (11, 16, 21, 26)
XD_PE, XD_ACT, CT_PE, CT_ACT = (27, 28), 32, 32, 35
DT_PE, DT_ACT, DT_DVE = (34, 36, 38, 41), (37, 38, 41, 44), (37, 38, 44, 45)
LN_ACT, DELTA_DVE, DU_GP = 49, (51, 52, 53, 54), (60, 61, 62, 63)
UD_PE, UD_ACT = (55, 57, 60, 61), (57, 60, 63, 68)
Z_PE, Z_ACT, Z_DVE = (44, 48, 50, 52), (47, 51, 52, 54), (46, 52, 53, 56)
PAIR, LAST_PAIR = (6, 38), 4
Y_PE, YG_DVE, O_PE, R1_DVE, POW1_GP, N1_DVE = 1, 2, (3, 4), 9, 13, 12
T_PE, T_ACT, X1B_GP, F1_PE, F1_ACT = 12, 15, 16, (17, 19, 21, 25), (20, 21, 26, 27)
F2_PE, R2_DVE, POW2_GP, N2_DVE, OUT_SP = (27, 28, 30, 31), 33, 42, 41, 39
XZ_SP, XR_SP = (20, 24), (54, 58)
SETUP = 20
ACC_DVE, SHARED_ACT, SHARED_GP = 1, 2, 5


def due(s, q, *tasks):
    for c, at in enumerate(tasks):
        if (q - at) % QS == 0:
            return s + (q - at) // QS, c
    return None


def due_prep(s, q, *tasks):
    found = due(s, q, *tasks)
    return (found[0] + 1, found[1]) if found and 0 <= found[0] + 1 < UNITS else None


def due_post(s, q, *tasks):
    found = []
    for w in (s - 2, s - 1):
        for p in range(2):
            start = PAIR[0] + LAST_PAIR if p and w == UNITS - 1 else PAIR[p]
            found += [(w, p, c) for c, at in enumerate(tasks) if QS * (s - 1 - w) + q == start + at]
    return [task for task in found if 0 <= task[0] < UNITS]


def shared_sums(g, n, t):
    return LT * (len(SHARED) * g + sum(m < n for m in SHARED)) + (t + 1 if n in SHARED else 0)


def own_sums(g, n, t):
    return LT * (len(OWN) * g + sum(m < n for m in OWN)) + (t + 1 if n in OWN else 0)


def build(nc, x_d, xT_d, winT_d, convw_d, convb_d, xpT_d, dtT_d, dtb_d, alog_d, dskip_d, woT_d, w1_d, b1_d, w2_d,
          b2_d, out_d):
    bscr_d = nc.dram_tensor("b_rows", [UNITS, NS, L], F32, kind="Internal").ap()
    x_rows = x_d.rearrange("b (h q t p) m -> (b h) q p t m", h=SEQ // L, t=2, p=P)
    out_rows = out_d.rearrange("b (h q t p) m -> (b h) q p t m", h=SEQ // L, t=2, p=P)
    xT_cols = xT_d.rearrange("(c p) l -> p c l", p=P)

    ctx = ExitStack()
    with ctx:
        def sb(name, shape):
            return ctx.enter_context(nc.sbuf_tensor(name, shape, F32))

        def ps(name, shape):
            return ctx.enter_context(nc.psum_tensor(name, shape, F32))

        def sem(name):
            return ctx.enter_context(nc.semaphore(name))

        winT = sb("winT", [P, MT, 2 * DI])
        xpT = sb("xpT", [P, KT, XR])
        dtT = sb("dtT", [RK + 1, DI])
        woT = sb("woT", [P, KT, DM])
        w1 = sb("w1", [P, MT, FW])
        w2 = sb("w2", [P, WT, DM])
        b1 = sb("b1", [P, WT])
        b2 = sb("b2", [P, DM])
        convw = sb("convw", [P, KT, TAPS])
        convb = sb("convb", [P, KT])
        A = sb("A", [P, KT, NS])
        dskip = sb("dskip", [P, KT])
        ident = sb("ident", [P, P])
        diagD = sb("diagD", [P, KT, P])
        one = sb("one", [P, 1])
        mhalf = sb("mhalf", [P, 2])
        ln1 = sb("ln1", [P, 1])
        xT = sb("xT", [P, MT, L])
        xs = sb("xs", [P, KT, HALO + L])
        cv = sb("cv", [P, 2, L])
        sg = sb("sg", [P, 2, L])
        u = sb("u", [P, KT, L])
        xd = sb("xd", [XR, L])
        dtl = sb("dtl", [RK + 1, L])
        sp_t = sb("sp_t", [P, KT, L])
        sp_w = sb("sp_w", [P, 2, L])
        delta = sb("delta", [P, 2, KT, L])
        du = sb("du", [P, 2, KT, L])
        ct = sb("ct", [P, 2, LT, NS])
        bbc = sb("bbc", [P, B_RING, L])
        dbu = sb("dbu", [P, DB_RING, L])
        h = sb("h", [P, H_RING, KT, L])
        state = sb("state", [P, QS])
        acc = sb("acc", [P, 2, LT, DI])
        prod = sb("prod", [P, T_RING, DI])
        zg = sb("zg", [P, 2, KT, PW])
        xTz = sb("xTz", [P, 2, MT, PW])
        xres = sb("xres", [P, 2, 2, DM])
        x1_all = sb("x1", [P, 2, DM])
        x1b_all = sb("x1b", [P, 2, DM])
        x1T_all = sb("x1T", [P, MT, PW])
        hid_all = sb("hid", [P, WT, PW])
        y2 = sb("y2", [P, 2, 2, DM])
        stats = sb("stats", [P, 2, 6])
        mv1 = sb("mv1", [P, 2, 2, 2])
        rs1 = sb("rs1", [P, 2, 2])
        mv2 = sb("mv2", [P, 2, 2, 2])
        rs2 = sb("rs2", [P, 2, 2])

        dA = [ps(f"dA{i}", [P, L]) for i in range(2)]
        hT = [ps(f"hT{i}", [P, DI]) for i in range(2)]
        pp = ps("pp", [P, 2, L])
        po_all = ps("po", [P, 2, 512])

        s_load = sem("s_load")
        s_load2 = sem("s_load2")
        s_load3 = sem("s_load3")
        s_const = sem("s_const")
        s_a = sem("s_a")
        s_chain = sem("s_chain")
        s_ach = sem("s_ach")
        s_xt = sem("s_xt")
        s_x = sem("s_x")
        s_halo = sem("s_halo")
        s_xs = sem("s_xs")
        s_c = sem("s_c")
        s_s = sem("s_s")
        s_u = sem("s_u")
        s_xd = sem("s_xd")
        s_xdc = sem("s_xdc")
        s_bs = sem("s_bs")
        s_ctp = sem("s_ctp")
        s_ct = sem("s_ct")
        s_dt = sem("s_dt")
        s_sp = sem("s_sp")
        s_spv = sem("s_spv")
        s_delta = sem("s_delta")
        s_du = sem("s_du")
        s_udp = sem("s_udp")
        s_ud = sem("s_ud")
        s_b = [sem(f"s_b{i}") for i in range(B_RING)]
        s_da = sem("s_da")
        s_db = sem("s_db")
        s_scan = sem("s_scan")
        s_save = sem("s_save")
        s_ht = sem("s_ht")
        s_acc = sem("s_acc")
        s_prod = sem("s_prod")
        s_shared = sem("s_shared")
        s_xz = [sem(f"s_xz{i}") for i in range(2)]
        s_xr = [sem(f"s_xr{i}") for i in range(2)]
        s_z = sem("s_z")
        s_ln = sem("s_ln")
        s_half = sem("s_half")
        s_var1 = [sem(f"s_var1{p}") for p in range(2)]
        s_rs1 = [sem(f"s_rs1{p}") for p in range(2)]
        s_var2 = [sem(f"s_var2{p}") for p in range(2)]
        s_rs2 = [sem(f"s_rs2{p}") for p in range(2)]
        s_zs = sem("s_zs")
        s_zg = sem("s_zg")
        s_yt = [sem(f"s_yt{p}") for p in range(2)]
        s_yg = [sem(f"s_yg{p}") for p in range(2)]
        s_o = [sem(f"s_o{p}") for p in range(2)]
        s_r1 = [sem(f"s_r1{p}") for p in range(2)]
        s_x1 = [sem(f"s_x1{p}") for p in range(2)]
        s_x1b = [sem(f"s_x1b{p}") for p in range(2)]
        s_tp = [sem(f"s_tp{p}") for p in range(2)]
        s_x1T = [sem(f"s_x1T{p}") for p in range(2)]
        s_f1 = [sem(f"s_f1{p}") for p in range(2)]
        s_hid = [sem(f"s_hid{p}") for p in range(2)]
        s_f2 = [sem(f"s_f2{p}") for p in range(2)]
        s_r2 = [sem(f"s_r2{p}") for p in range(2)]
        s_y2 = [sem(f"s_y2{p}") for p in range(2)]
        s_out = [sem(f"s_out{i}") for i in range(2)]

        def buffers(w, p):
            if (w, p) == (UNITS - 1, 1):
                return (pp, *[sp_t[:, c, :].rearrange("p (t m) -> p t m", t=2) for c in range(3)],
                        u[:].rearrange("p k (a l) -> p (k a) l", a=2))
            return po_all, x1_all[:], x1b_all[:], x1T_all[:], hid_all[:]

        def pair_before(w, p):
            return 0 if (w, p) == (UNITS - 1, 1) else w + p

        def has_main(s):
            return 0 <= s < UNITS

        def has_prep(s):
            return s + 1 < UNITS

        block = ctx.enter_context(nc.Block())
        LOADS, LOADS2, LOADS3 = 16 * 3, 16 * 5, 16 * 6

        @block.sync
        def _(sp):
            sp.dma_start(xT[:], xT_cols[:, :, 0:L]).then_inc(s_xt, 16)
            sp.dma_start(winT[:, :, 0:DI], winT_d.rearrange("(c p) n -> p c n", p=P)[:, :, 0:DI]).then_inc(s_load, 16)
            sp.dma_start(convw[:], convw_d.rearrange("(k p) a t -> p k (a t)", p=P)).then_inc(s_load, 16)
            sp.dma_start(convb[:], convb_d).then_inc(s_load, 16)
            sp.dma_start(dskip[:], dskip_d).then_inc(s_load2, 16)
            sp.dma_start(A[:], alog_d.rearrange("(k p) n -> p k n", p=P)).then_inc(s_load2, 16)
            sp.dma_start(xpT[:], xpT_d.rearrange("(k p) n -> p k n", p=P)).then_inc(s_load2, 16)
            sp.dma_start(dtT[0:RK, :], dtT_d).then_inc(s_load2, 16)
            sp.dma_start(dtT[RK:RK + 1, :], dtb_d.rearrange("(a n) -> a n", a=1)).then_inc(s_load2, 16)
            sp.dma_start(winT[:, :, DI:], winT_d.rearrange("(c p) n -> p c n", p=P)[:, :, DI:]).then_inc(s_load3, 16)
            sp.dma_start(woT[:], woT_d.rearrange("(k p) n -> p k n", p=P)).then_inc(s_load3, 16)
            sp.dma_start(w1[:], w1_d.rearrange("(c p) n -> p c n", p=P)).then_inc(s_load3, 16)
            sp.dma_start(b1[:], b1_d).then_inc(s_load3, 16)
            sp.dma_start(w2[:], w2_d.rearrange("(w p) n -> p w n", p=P)).then_inc(s_load3, 16)
            sp.dma_start(b2[:], b2_d.rearrange("(a n) -> a n", a=1).broadcast_to([P, DM])).then_inc(s_load3, 16)

            def load_b(t):
                g, n = divmod(t, NS)
                if t >= B_RING:
                    sp.wait_ge(s_db, KT * (t - B_RING + 1))
                if n == 0:
                    sp.wait_ge(s_bs, 16 * (g + 1))
                sp.dma_start(bbc[:, t % B_RING, :], bscr_d[g, n:n + 1, :].broadcast_to([P, L])).then_inc(
                    s_b[t % B_RING], 16)

            for s in range(-1, UNITS + 2):
                for q in range(QS):
                    n, k = divmod(q, KT)
                    if (task := due_prep(s, q, X_PE[-1] + 2)) and task[0] + 1 < UNITS:
                        v = task[0]
                        sp.wait_ge(s_x, KT * (v + 1))
                        sp.dma_start(xT[:], xT_cols[:, :, (v + 1) * L:(v + 2) * L]).then_inc(s_xt, 16)
                    if task := due_prep(s, q, XD_ACT + 1):
                        v = task[0]
                        sp.wait_ge(s_xdc, 2 * (v + 1))
                        sp.dma_start(bscr_d[v], xd[RK:RK + NS, :]).then_inc(s_bs, 16)
                    ahead = NS * s + n + B_RING - 1
                    if k == 0 and 0 <= ahead < UNITS * NS and s < UNITS:
                        load_b(ahead)
                    if has_main(s) and q in XZ_SP:
                        p = XZ_SP.index(q)
                        if s >= 1:
                            sp.wait_ge(s_z, 4 * (s - 1) + 2 * (p + 1))
                        at = s * L + p * PW
                        sp.dma_start(xTz[:, p], xT_cols[:, :, at:at + PW]).then_inc(s_xz[p], 16)
                    if has_main(s) and q in XR_SP:
                        p = XR_SP.index(q)
                        if s >= 1:
                            sp.wait_ge(s_r1[p], s)
                        sp.dma_start(xres[:, p], x_rows[s, p]).then_inc(s_xr[p], 16)
                    for w, p, _ in due_post(s, q, OUT_SP):
                        sp.wait_ge(s_y2[p], 2 * (w + 1))
                        sp.dma_start(out_rows[w, p], y2[:, p]).then_inc(s_out[p], 16)
            for p in range(2):
                sp.wait_ge(s_out[p], 16 * UNITS)

        @block.gpsimd
        def _(gp):
            nc.gpsimd.memset(ident[:], 0.0).then_inc(s_a, 1)
            nc.gpsimd.memset(dtl[:], 2.0).then_inc(s_const, 1)
            nc.gpsimd.memset(one[:], 1.0).then_inc(s_const, 1)
            nc.gpsimd.memset(mhalf[:], -0.5).then_inc(s_const, 1)
            gp.wait_ge(s_a, 1)
            nc.gpsimd.affine_select(out=ident[:], in_=ident[:], compare_op=ALU.not_equal, fill=1.0, base=0,
                                    pattern=[[-1, P]], channel_multiplier=1).then_inc(s_const, 1)
            for s in range(-1, UNITS + 2):
                for q in range(QS):
                    n, k = divmod(q, KT)
                    if has_main(s):
                        i, t = QS * s + q, NS * s + n
                        if k == 0:
                            gp.wait_ge(s_b[t % B_RING], 16 * (t // B_RING + 1))
                        if n == 0:
                            gp.wait_ge(s_du, KT * s + k + 1)
                        if i >= DB_RING:
                            gp.wait_ge(s_scan, i - DB_RING + 1)
                        nc.gpsimd.tensor_tensor(dbu[:, i % DB_RING, :], du[:, s % 2, k, :], bbc[:, t % B_RING, :],
                                                ALU.mult).then_inc(s_db, 1)
                    m, t = divmod(q - KT - SHARED_GP, LT)
                    if has_main(s) and m in SHARED:
                        i = shared_sums(s, m, t)
                        gp.wait_ge(s_prod, i)
                        gp.wait_ge(s_acc, own_sums(s, m, t) - LT + t + 1)
                        nc.gpsimd.tensor_tensor(acc[:, s % 2, t, :], acc[:, s % 2, t, :], prod[:, (i - 1) % T_RING, :],
                                                ALU.add).then_inc(s_shared, 1)
                    if (task := due_prep(s, q, *DU_GP)) and task[0]:
                        v, c = task
                        gp.wait_ge(s_delta, KT * v + c + 1)
                        nc.gpsimd.tensor_tensor(du[:, v % 2, c, :], delta[:, v % 2, c, :], u[:, c, :],
                                                ALU.mult).then_inc(s_du, 1)
                    for w, p, _ in due_post(s, q, POW1_GP):
                        gp.wait_ge(s_var1[p], w + 1)
                        nc.gpsimd.tensor_tensor(rs1[:, p], rs1[:, p], mhalf[:], ALU.pow).then_inc(s_rs1[p], 1)
                    for w, p, _ in due_post(s, q, X1B_GP):
                        gp.wait_ge(s_x1[p], 2 * (w + 1))
                        if before := pair_before(w, p):
                            gp.wait_ge(s_y2[1 - p], 2 * before)
                        gp.wait_ge(s_load3, LOADS3)
                        x1, x1b = buffers(w, p)[1:3]
                        nc.gpsimd.tensor_tensor(x1b, x1, b2[:].unsqueeze(1).broadcast_to([P, 2, DM]),
                                                ALU.add).then_inc(s_x1b[p], 1)
                    for w, p, _ in due_post(s, q, POW2_GP):
                        gp.wait_ge(s_var2[p], w + 1)
                        nc.gpsimd.tensor_tensor(rs2[:, p], rs2[:, p], mhalf[:], ALU.pow).then_inc(s_rs2[p], 1)

        @block.scalar
        def _(act):
            own = [0]

            def link(ins):
                own[0] += 1
                ins.then_inc(s_ach, 1)
                act.wait_ge(s_ach, own[0])

            act.wait_ge(s_const, 4)
            nc.scalar.activation(ln1[:], one[:], ACT.Tanh)
            act.wait_ge(s_half, 2)
            for s in range(-1, UNITS + 2):
                for q in range(QS):
                    n, k = divmod(q, KT)
                    if has_main(s):
                        i = QS * s + q
                        if n == 0:
                            act.wait_ge(s_delta, KT * s + k + 1)
                        if i >= 2:
                            act.wait_ge(s_scan, i - 1)
                        nc.scalar.activation(dA[i % 2][:, :], delta[:, s % 2, k, :], ACT.Exp,
                                             scale=A[:, k, n:n + 1]).then_inc(s_da, 1)
                        m, t = divmod(q - KT - SHARED_ACT, LT)
                        if m in SHARED:
                            i = shared_sums(s, m, t)
                            act.wait_ge(s_ht, QS * s + KT * m + t + 1)
                            if i > T_RING:
                                act.wait_ge(s_shared, i - T_RING)
                            if m == SHARED[0] and t == 0:
                                act.wait_ge(s_ct, s + 1)
                            nc.scalar.activation(prod[:, (i - 1) % T_RING, :], hT[t % 2][:, :], ACT.Copy,
                                                 scale=ct[:, s % 2, t, m:m + 1]).then_inc(s_prod, 1)
                    if task := due_prep(s, q, *X_ACT):
                        v, c = task
                        act.wait_ge(s_x, KT * v + c + 1)
                        act.wait_ge(s_halo, v + 1)
                        if KT * v + c >= 2:
                            act.wait_ge(s_u, KT * v + c - 1)
                        nc.scalar.activation(xs[:, c, HALO:], pp[:, c % 2, :], ACT.Copy).then_inc(s_xs, 1)
                        nc.scalar.activation(cv[:, c % 2, :], pp[:, c % 2, :], ACT.Identity,
                                             bias=convb[:, c:c + 1],
                                             scale=convw[:, c, HALO:TAPS]).then_inc(s_xs, 1)
                    if task := due_prep(s, q, *X_TANH):
                        v, c = task
                        act.wait_ge(s_c, KT * v + c + 1)
                        nc.scalar.activation(sg[:, c % 2, :], cv[:, c % 2, :], ACT.Tanh).then_inc(s_s, 1)
                    if s == -1 and q == SETUP:
                        act.wait_ge(s_load2, LOADS2)
                        link(nc.scalar.activation(A[:], A[:], ACT.Exp))
                        link(nc.scalar.activation(A[:], A[:], ACT.Copy, scale=-1.0))
                    if task := due_prep(s, q, XD_ACT):
                        v = task[0]
                        act.wait_ge(s_xd, v + 1)
                        if v >= 1:
                            act.wait_ge(s_bs, 16 * v)
                        nc.scalar.activation(xd[:, :], pp[0:XR, 0, :], ACT.Copy).then_inc(s_xdc, 1)
                        nc.scalar.activation(dtl[0:RK, :], pp[0:RK, 0, :], ACT.Copy).then_inc(s_xdc, 1)
                    if task := due_prep(s, q, CT_ACT):
                        v = task[0]
                        act.wait_ge(s_ctp, v + 1)
                        nc.scalar.activation(
                            ct[:, v % 2], pp[:, 1, 0:LT * XR].rearrange("p (t r) -> p t r", r=XR)[:, :, RK + NS:XR],
                            ACT.Copy).then_inc(s_ct, 1)
                    if task := due_prep(s, q, *DT_ACT):
                        v, c = task
                        m = KT * v + c
                        act.wait_ge(s_dt, m + 1)
                        if v:
                            act.wait_ge(s_delta, KT * v)
                        if m >= 2:
                            act.wait_ge(s_spv, 2 * (m - 1))
                        link(nc.scalar.activation(sp_t[:, c, :], pp[:, c % 2, :], ACT.Abs))
                        link(nc.scalar.activation(sp_t[:, c, :], sp_t[:, c, :], ACT.Exp, scale=-1.0))
                        nc.scalar.activation(sp_w[:, c % 2, :], sp_t[:, c, :], ACT.Identity,
                                             bias=one[:, 0:1]).then_inc(s_sp, 1)
                    if task := due_prep(s, q, LN_ACT):
                        v = task[0]
                        if v == 0:
                            link(nc.scalar.activation(ln1[:], one[:], ACT.Ln))
                        act.wait_ge(s_spv, 2 * KT * (v + 1))
                        nc.scalar.activation(sp_t[:], sp_t[:], ACT.Ln, bias=one[:, 0:1]).then_inc(s_ln, 1)
                    if task := due_prep(s, q, *UD_ACT):
                        v, t = task
                        act.wait_ge(s_udp, LT * v + t + 1)
                        if v >= 2:
                            act.wait_ge(s_yt[1], v - 1)
                        nc.scalar.activation(acc[:, v % 2, t, :], pp[:, t % 2, :], ACT.Copy).then_inc(s_ud, 1)
                    if has_main(s) and q in Z_ACT:
                        p, b = divmod(Z_ACT.index(q), 2)
                        act.wait_ge(s_z, 4 * s + 2 * p + b + 1)
                        if s >= 1:
                            act.wait_ge(s_o[p], s)
                        nc.scalar.activation(zg[:, p, 2 * b:2 * b + 2, :].rearrange("p k l -> p (k l)"), pp[:, b, :],
                                             ACT.Tanh, scale=0.5).then_inc(s_zs, 1)
                    for w, p, _ in due_post(s, q, T_ACT):
                        act.wait_ge(s_tp[p], w + 1)
                        po, _, _, x1T, _ = buffers(w, p)
                        nc.scalar.activation(x1T.rearrange("p c l -> p (c l)"), po[:, 1, :],
                                             ACT.Copy).then_inc(s_x1T[p], 1)
                    for w, p, f in due_post(s, q, *F1_ACT):
                        act.wait_ge(s_f1[p], 4 * w + f + 1)
                        po, _, _, _, hid = buffers(w, p)
                        for a in range(2):
                            nc.scalar.activation(hid[:, 2 * f + a, :], po[:, f % 2, a * PW:(a + 1) * PW], ACT.Relu,
                                                 bias=b1[:, 2 * f + a:2 * f + a + 1]).then_inc(s_hid[p], 1)

        @block.vector
        def _(dve):
            own = [0]

            def link(ins):
                own[0] += 1
                ins.then_inc(s_chain, 1)
                dve.wait_ge(s_chain, own[0])

            def accumulate(g, n, t):
                dve.wait_ge(s_ht, QS * g + LT * n + t + 1)
                if n == 0:
                    dve.wait_ge(s_ud, LT * g + t + 1)
                    dve.wait_ge(s_ct, g + 1)
                elif n - 1 in SHARED:
                    dve.wait_ge(s_shared, shared_sums(g, n - 1, t))
                else:
                    dve.wait_ge(s_acc, own_sums(g, n - 1, t))
                nc.vector.scalar_tensor_tensor(out=acc[:, g % 2, t, :], in0=hT[t % 2][:, :],
                                               scalar=ct[:, g % 2, t, n:n + 1], in1=acc[:, g % 2, t, :],
                                               op0=ALU.mult, op1=ALU.add).then_inc(s_acc, 1)

            def row_moments(src, mv, rs, s_var):
                nc.vector.bn_stats(stats[:, 0, :], src[:, 0, :])
                link(nc.vector.bn_stats(stats[:, 1, :], src[:, 1, :]))
                nc.vector.bn_aggr(mv[:, 0, :], stats[:, 0, :])
                link(nc.vector.bn_aggr(mv[:, 1, :], stats[:, 1, :]))
                nc.vector.tensor_scalar(rs, mv[:, :, 1], EPS, None, ALU.add).then_inc(s_var, 1)

            def normalize(out, src, mv, rs, s_out):
                for t in range(2):
                    nc.vector.tensor_scalar(out[:, t, :], src[:, t, :], mv[:, t, 0:1], rs[:, t:t + 1],
                                            ALU.subtract, ALU.mult).then_inc(s_out, 1)

            dve.wait_ge(s_load, LOADS)
            nc.vector.tensor_scalar(convw[:], convw[:], 0.5, None, ALU.mult).then_inc(s_half, 1)
            nc.vector.tensor_scalar(convb[:], convb[:], 0.5, None, ALU.mult).then_inc(s_half, 1)
            dve.wait_ge(s_half, 2)
            for s in range(-1, UNITS + 2):
                v = s + 1
                if has_prep(s):
                    if v % 2 == 0:
                        if v:
                            dve.wait_ge(s_c, KT * v)
                        nc.vector.memset(xs[:, :, 0:HALO], 0.0).then_inc(s_halo, 1)
                    else:
                        dve.wait_ge(s_xs, 2 * KT * v)
                        nc.vector.tensor_copy(xs[:, :, 0:HALO], xs[:, :, L:L + HALO]).then_inc(s_halo, 1)
                for q in range(QS):
                    n, k = divmod(q, KT)
                    if has_main(s):
                        i = QS * s + q
                        dve.wait_ge(s_da, i + 1)
                        dve.wait_ge(s_db, i + 1)
                        state_no = NS * s + n
                        if state_no >= H_RING:
                            dve.wait_ge(s_ht, LT * (state_no - H_RING + 1))
                        first = s % 2 == 0
                        if not first:
                            dve.wait_ge(s_save, NS * (s // 2) + n + 1)
                        nc.vector.tensor_tensor_scan(h[:, state_no % H_RING, k, :], dA[i % 2][:, :], dbu[:, i % DB_RING, :],
                                                     0.0 if first else state[:, KT * n + k:KT * n + k + 1],
                                                     ALU.mult, ALU.add).then_inc(s_scan, 1)
                    m, g = (n - 1, s) if n else (NS - 1, s - 1)
                    if has_main(g):
                        if k == 0 and g % 2 == 0:
                            dve.wait_ge(s_scan, QS * g + KT * (m + 1))
                            nc.vector.tensor_copy(state[:, KT * m:KT * (m + 1)].unsqueeze(2),
                                                  h[:, (NS * g + m) % H_RING, :, L - 1:L]).then_inc(s_save, 1)
                    g, j = divmod(QS * s + q - KT - ACC_DVE, QS)
                    m, t = divmod(j, LT)
                    if has_main(g) and m in OWN:
                        accumulate(g, m, t)
                    if s == -1 and q == SETUP:
                        dve.wait_ge(s_load2, LOADS2)
                        dve.wait_ge(s_const, 4)
                        for c in range(KT):
                            nc.vector.tensor_scalar(diagD[:, c, :], ident[:], dskip[:, c:c + 1], None,
                                                    ALU.mult).then_inc(s_const, 1)
                    if s == 0 and q == SETUP:
                        dve.wait_ge(s_load3, LOADS3)
                        nc.vector.tensor_scalar(woT[:], woT[:], 0.5, None, ALU.mult).then_inc(s_half, 1)
                    if task := due_prep(s, q, *X_DVE):
                        v, c = task
                        dve.wait_ge(s_xs, 2 * (KT * v + c + 1))
                        dve.wait_ge(s_halo, v + 1)
                        for j in range(1, TAPS):
                            tap = (nc.vector.scalar_tensor_tensor(
                                out=cv[:, c % 2, :], in0=xs[:, c, HALO - j:HALO - j + L],
                                scalar=convw[:, c, HALO - j:TAPS - j], in1=cv[:, c % 2, :],
                                op0=ALU.mult, op1=ALU.add))
                            if j < HALO:
                                link(tap)
                        tap.then_inc(s_c, 1)
                    if task := due_prep(s, q, *U_DVE):
                        v, c = task
                        dve.wait_ge(s_s, KT * v + c + 1)
                        if v:
                            dve.wait_ge(s_udp, LT * v)
                        nc.vector.scalar_tensor_tensor(out=u[:, c, :], in0=sg[:, c % 2, :], scalar=1.0,
                                                       in1=cv[:, c % 2, :], op0=ALU.add,
                                                       op1=ALU.mult).then_inc(s_u, 1)
                    if task := due_prep(s, q, *DT_DVE):
                        v, c = task
                        m1 = KT * v + c
                        dve.wait_ge(s_sp, m1 + 1)
                        nc.vector.scalar_tensor_tensor(out=sp_w[:, c % 2, :], in0=sp_w[:, c % 2, :], scalar=1.0,
                                                       in1=sp_t[:, c, :], op0=ALU.subtract,
                                                       op1=ALU.subtract).then_inc(s_spv, 1)
                        dve.wait_ge(s_spv, 2 * m1 + 1)
                        nc.vector.scalar_tensor_tensor(out=delta[:, v % 2, c, :], in0=pp[:, c % 2, :], scalar=0.0,
                                                       in1=sp_w[:, c % 2, :], op0=ALU.max,
                                                       op1=ALU.subtract).then_inc(s_spv, 1)
                    if task := due_prep(s, q, *DELTA_DVE):
                        v, c = task
                        dve.wait_ge(s_ln, v + 1)
                        dve.wait_ge(s_spv, 2 * (KT * v + c + 1))
                        nc.vector.scalar_tensor_tensor(out=delta[:, v % 2, c, :], in0=sp_t[:, c, :], scalar=ln1[:, 0:1],
                                                       in1=delta[:, v % 2, c, :], op0=ALU.subtract,
                                                       op1=ALU.add).then_inc(s_delta, 1)
                        if v == 0:
                            dve.wait_ge(s_delta, c + 1)
                            nc.vector.tensor_tensor(du[:, 0, c, :], delta[:, 0, c, :], u[:, c, :],
                                                    ALU.mult).then_inc(s_du, 1)
                    if has_main(s) and q in Z_DVE:
                        p, b = divmod(Z_DVE.index(q), 2)
                        dve.wait_ge(s_zs, 4 * s + 2 * p + b + 1)
                        half = zg[:, p, 2 * b:2 * b + 2, :].rearrange("p k l -> p (k l)")
                        nc.vector.scalar_tensor_tensor(out=half, in0=half, scalar=1.0, in1=pp[:, b, :], op0=ALU.add,
                                                       op1=ALU.mult).then_inc(s_zg, 1)
                    for w, p, _ in due_post(s, q, YG_DVE):
                        po = buffers(w, p)[0]
                        dve.wait_ge(s_yt[p], w + 1)
                        dve.wait_ge(s_zg, 2 * (2 * w + p + 1))
                        nc.vector.tensor_tensor(zg[:, p].rearrange("p k l -> p (k l)"),
                                                po[:, :, :].rearrange("p a l -> p (a l)"),
                                                zg[:, p].rearrange("p k l -> p (k l)"), ALU.mult).then_inc(s_yg[p], 1)
                    for w, p, _ in due_post(s, q, R1_DVE):
                        po, x1 = buffers(w, p)[:2]
                        dve.wait_ge(s_o[p], w + 1)
                        if before := pair_before(w, p):
                            dve.wait_ge(s_x1b[1 - p], before)
                            dve.wait_ge(s_tp[1 - p], before)
                        dve.wait_ge(s_xr[p], 16 * (w + 1))
                        nc.vector.tensor_tensor(x1.rearrange("p t m -> p (t m)"), po[:, 0, :],
                                                xres[:, p].rearrange("p t m -> p (t m)"), ALU.add).then_inc(s_r1[p], 1)
                        dve.wait_ge(s_r1[p], w + 1)
                        row_moments(x1, mv1[:, p], rs1[:, p], s_var1[p])
                    for w, p, _ in due_post(s, q, N1_DVE):
                        x1 = buffers(w, p)[1]
                        dve.wait_ge(s_rs1[p], w + 1)
                        normalize(x1, x1, mv1[:, p], rs1[:, p], s_x1[p])
                    for w, p, _ in due_post(s, q, R2_DVE):
                        po, _, x1b = buffers(w, p)[:3]
                        dve.wait_ge(s_f2[p], w + 1)
                        dve.wait_ge(s_x1b[p], w + 1)
                        nc.vector.tensor_tensor(x1b.rearrange("p t m -> p (t m)"), po[:, 0, :],
                                                x1b.rearrange("p t m -> p (t m)"), ALU.add).then_inc(s_r2[p], 1)
                        dve.wait_ge(s_r2[p], w + 1)
                        row_moments(x1b, mv2[:, p], rs2[:, p], s_var2[p])
                    for w, p, _ in due_post(s, q, N2_DVE):
                        dve.wait_ge(s_rs2[p], w + 1)
                        if w >= 1:
                            dve.wait_ge(s_out[p], 16 * w)
                        normalize(y2[:, p], buffers(w, p)[2], mv2[:, p], rs2[:, p], s_y2[p])

        @block.tensor
        def _(pe):
            def mm(out, lhsT, rhs, start=True, stop=True):
                return nc.tensor.matmul(out, lhsT, rhs, start=start, stop=stop)

            pe.wait_ge(s_load, LOADS)
            for s in range(-1, UNITS + 2):
                for q in range(QS):
                    n, t = divmod(q, LT)
                    g, m = (s, n - 1) if n else (s - 1, NS - 1)
                    if has_main(g):
                        j = QS * g + LT * m + t
                        pe.wait_ge(s_scan, QS * g + KT * (m + 1))
                        if j >= 2:
                            before = divmod(j - 2, QS)
                            before = (before[0], *divmod(before[1], LT))
                            if before[1] in SHARED:
                                pe.wait_ge(s_prod, shared_sums(*before))
                            else:
                                pe.wait_ge(s_acc, own_sums(*before))
                        for c in range(KT):
                            last = nc.tensor.transpose(hT[t % 2][:, c * P:(c + 1) * P],
                                                       h[:, (NS * g + m) % H_RING, c, t * P:(t + 1) * P], ident[:])
                        last.then_inc(s_ht, 1)
                    if task := due_prep(s, q, *X_PE):
                        v, c = task
                        if c == 0:
                            pe.wait_ge(s_xt, 16 * (v + 1))
                        if c >= 2:
                            pe.wait_ge(s_xs, 2 * (KT * v + c - 1))
                        elif v:
                            pe.wait_ge(s_ud, LT * v - 1 + c)
                        for a in range(MT):
                            last = mm(pp[:, c % 2, :], winT[:, a, c * P:(c + 1) * P], xT[:, a, :],
                                      a == 0, a == MT - 1)
                        last.then_inc(s_x, 1)
                    if task := due_prep(s, q, *XD_PE):
                        v, b = task
                        if b == 0:
                            pe.wait_ge(s_xs, 2 * KT * (v + 1))
                        if v == 0:
                            pe.wait_ge(s_load2, LOADS2)
                            pe.wait_ge(s_const, 4 + KT)
                        pe.wait_ge(s_u, KT * v + 2 * (b + 1))
                        for c in (2 * b, 2 * b + 1):
                            last = mm(pp[0:XR, 0, :], xpT[:, c, :], u[:, c, :], c == 0, c == KT - 1)
                        if b:
                            last.then_inc(s_xd, 1)
                    if task := due_prep(s, q, CT_PE):
                        v = task[0]
                        pe.wait_ge(s_xdc, 2 * (v + 1))
                        for t in range(LT):
                            last = nc.tensor.transpose(pp[:, 1, t * XR:(t + 1) * XR], xd[:, t * P:(t + 1) * P],
                                                       ident[0:XR, 0:XR])
                        last.then_inc(s_ctp, 1)
                    if task := due_prep(s, q, *DT_PE):
                        v, c = task
                        if c == 1:
                            pe.wait_ge(s_ct, v + 1)
                        if c >= 2:
                            pe.wait_ge(s_spv, 2 * (KT * v + c - 1))
                        mm(pp[:, c % 2, :], dtT[:, c * P:(c + 1) * P], dtl[:, :]).then_inc(s_dt, 1)
                    if has_main(s) and q in Z_PE:
                        p, b = divmod(Z_PE.index(q), 2)
                        if b == 0:
                            pe.wait_ge(s_xz[p], 16 * (s + 1))
                        if s == 0:
                            pe.wait_ge(s_load3, LOADS3)
                        if p:
                            pe.wait_ge(s_zg, 4 * s + b + 1)
                        elif has_prep(s):
                            pe.wait_ge(s_spv, 2 * (KT * (s + 1) + 3 + b))
                        else:
                            pe.wait_ge(s_ud, LT * UNITS)
                        for c in (2 * b, 2 * b + 1):
                            for a in range(MT):
                                last = mm(pp[:, b, (c % 2) * PW:(c % 2 + 1) * PW],
                                          winT[:, a, DI + c * P:DI + (c + 1) * P], xTz[:, p, a, :],
                                          a == 0, a == MT - 1)
                        last.then_inc(s_z, 1)
                    if task := due_prep(s, q, *UD_PE):
                        v, t = task
                        if t >= 2:
                            pe.wait_ge(s_ud, LT * v + t - 1)
                        elif v:
                            pe.wait_ge(s_zg, 4 * (v - 1) + 3 + t)
                        else:
                            pe.wait_ge(s_spv, 2 * (KT * v + 3 + t))
                        for c in range(KT):
                            last = mm(pp[:, t % 2, c * P:(c + 1) * P], u[:, c, t * P:(t + 1) * P], diagD[:, c, :])
                        last.then_inc(s_udp, 1)
                    for w, p, _ in due_post(s, q, Y_PE):
                        po = buffers(w, p)[0]
                        pe.wait_ge(s_acc, own_sums(w, NS - 1, 2 * p + 1))
                        pe.wait_ge(s_shared, shared_sums(w, NS - 1, 2 * p + 1))
                        if before := pair_before(w, p):
                            pe.wait_ge(s_r2[1 - p], before)
                        elif w:
                            pe.wait_ge(s_zg, 4 * UNITS)
                        for c in range(KT):
                            for t in range(2):
                                last = nc.tensor.transpose(
                                    po[:, c // 2, (c % 2) * PW + t * P:(c % 2) * PW + (t + 1) * P],
                                    acc[:, w % 2, 2 * p + t, c * P:(c + 1) * P], ident[:])
                        last.then_inc(s_yt[p], 1)
                    for w, p, t in due_post(s, q, *O_PE):
                        po = buffers(w, p)[0]
                        pe.wait_ge(s_yg[p], w + 1)
                        pe.wait_ge(s_half, 3)
                        for c in range(KT):
                            last = mm(po[:, 0, t * DM:(t + 1) * DM], zg[:, p, c, t * P:(t + 1) * P],
                                      woT[:, c, :], c == 0, c == KT - 1)
                        if t:
                            last.then_inc(s_o[p], 1)
                    for w, p, _ in due_post(s, q, T_PE):
                        po, x1 = buffers(w, p)[:2]
                        pe.wait_ge(s_x1[p], 2 * (w + 1))
                        for a in range(MT):
                            for t in range(2):
                                last = nc.tensor.transpose(po[:, 1, a * PW + t * P:a * PW + (t + 1) * P],
                                                           x1[:, t, a * P:(a + 1) * P], ident[:])
                        last.then_inc(s_tp[p], 1)
                    for w, p, f in due_post(s, q, *F1_PE):
                        po, _, _, x1T, _ = buffers(w, p)
                        if f < 2:
                            pe.wait_ge(s_x1T[p], w + 1)
                        else:
                            pe.wait_ge(s_hid[p], WT * w + 2 * (f - 1))
                        for a in range(2):
                            for c in range(MT):
                                at_w = (2 * f + a) * P
                                last = mm(po[:, f % 2, a * PW:(a + 1) * PW], w1[:, c, at_w:at_w + P],
                                          x1T[:, c, :], c == 0, c == MT - 1)
                        last.then_inc(s_f1[p], 1)
                    for w, p, b in due_post(s, q, *F2_PE):
                        t, b = divmod(b, 2)
                        po, _, _, _, hid = buffers(w, p)
                        pe.wait_ge(s_hid[p], WT * (w + 1) - (0 if t or b else 2))
                        for a in range(4 * b, 4 * b + 4):
                            last = mm(po[:, 0, t * DM:(t + 1) * DM], hid[:, a, t * P:(t + 1) * P],
                                      w2[:, a, :], a == 0, a == WT - 1)
                        if t and b:
                            last.then_inc(s_f2[p], 1)


def kernel(**inputs):
    import concourse.bacc as bacc
    from concourse.bass_utils import run_bass_kernel_spmd

    get = {name: np.asarray(a) for name, a in inputs.items()}
    x = get["L0_attn_hidden_states"]
    arrays = {
        "x": x,
        "xT": x.reshape(BATCH * SEQ, DM).T,
        "winT": get["L0_attn_in_proj_w"].T,
        "conv_w": get["L0_attn_conv_w"],
        "conv_b": get["L0_attn_conv_b"],
        "xpT": get["L0_attn_x_proj_w"].T,
        "dtT": get["L0_attn_dt_proj_w"].T,
        "dt_b": get["L0_attn_dt_proj_b"],
        "A_log": get["L0_attn_A_log"],
        "D": get["L0_attn_D"],
        "woT": get["L0_attn_out_proj_w"].T,
        "w1": get["L0_ffn_w1"],
        "b1": get["L0_ffn_b1"],
        "w2": get["L0_ffn_w2"],
        "b2": get["L0_ffn_b2"],
    }
    for name in ("conv_b", "D", "b1"):
        arrays[name] = arrays[name].reshape(-1, P).T
    arrays = {f"in_{name}": np.ascontiguousarray(a) for name, a in arrays.items()}
    nc = bacc.Bacc("TRN2", target_bir_lowering=False, num_devices=1)
    args = [nc.dram_tensor(name, a.shape, mybir.dt.from_np(a.dtype), kind="ExternalInput").ap()
            for name, a in arrays.items()]
    out = nc.dram_tensor("out", x.shape, F32, kind="ExternalOutput").ap()
    build(nc, *args, out)
    r = run_bass_kernel_spmd(nc, [arrays], core_ids=[0])
    return r.results[0]["out"]
```

```python
import numpy as np
import concourse.bass as bass
from concourse import mybir
from contextlib import ExitStack

F32 = mybir.dt.float32
ALU = mybir.AluOpType
ACT = mybir.ActivationFunctionType

P = 128
BATCH, SEQ, DM = 4, 1024, 256
DI, NS, RK, TAPS = 512, 16, 16, 4
FW = 1024
L = 512
UNITS = BATCH * SEQ // L
LAST = UNITS - 1
KT = DI // P
MT = DM // P
LT = L // P
HL = L // 2
WT = FW // P
XR = RK + 2 * NS
PW = 2 * P
QS = NS * KT
EPS = 1e-5
HALO = TAPS - 1
B_RING, DB_RING, H_RING = 4, 4, 3

SHARED = (1, 4, 8, 11)
T_RING = 3

X_PE, X_ACT, X_DVE, X_TANH, U_DVE = (1, 5, 12, 13), (4, 7, 15, 16), (5, 10, 16), (9, 12, 19, 22), (13, 16, 21, 25)
PE_TILES, CONV_PE, CV_ACT = (3,), (17,), (20,)
VE_TILES = tuple(c for c in range(KT) if c not in PE_TILES)
XD_PE, XD_ACT, CT_PE, CT_ACT = (25, 27), 32, 31, 33
DT_PE, DT_ACT, DT_DVE = (32, 35, 36, 39), (35, 37, 42, 46), (35, 37, 44, 45)
LN_ACT, DELTA_DVE, DU_GP = 47, (50, 51, 52, 53), (58, 62, 63, 64)
UD_PE, UD_ACT = (54, 58, 59, 60), (59, 61, 62, 69)
FIRST_X_PE, FIRST_X_ACT, FIRST_X_DVE, FIRST_X_TANH = (0, 1, 2, 3), (0, 1, 2, 3), (0, 1, 2), (5, 6, 7, 8)
FIRST_CONV_PE, FIRST_CV_ACT, FIRST_U_DVE = (4,), (7,), (5, 6, 7, 8)
FIRST_DT_PE, FIRST_DT_ACT, FIRST_DT_DVE = (36, 37, 38, 39), (36, 37, 38, 39), (36, 37, 38, 39)
Z_PE, Z_ACT, Z_DVE = (45, 47, 51, 53), (49, 52, 54, 57), (50, 52, 53, 56)
PAIR = (5, 37)
LAST_PAIRS = (25, -19, 4)
LAST_Z, LAST_XR = 34, 35
Y_PE, YG_DVE, O_PE, R1_DVE, POW1_GP, N1_ACT = 1, 2, (3, 5), 9, 11, 11
T_PE, T_ACT, F1_PE, F1_ACT = 11, 16, (15, 17, 20, 25), (20, 21, 27, 29)
F2_PE, R2_DVE, POW2_GP, N2_ACT, OUT_SP = (27, 28, 30, 31), 33, 38, 40, 39
XZ_SP, XR_SP = (37, 49), (52, 53)
SETUP = 20
ACC_DVE, SHARED_ACT, SHARED_GP = 1, 2, 5


def due_prep(s, q, *tasks, first=None):
    for v in (s, s + 1):
        for c, at in enumerate(first if first and v == 0 else tasks):
            if 0 <= v < UNITS and QS * (s + 1 - v) + q == at:
                return v, c
    return None


def due_gate(s, q, *tasks):
    for g in (s, s + 1):
        for c, at in enumerate(tasks):
            if 0 <= g < UNITS and QS * (s - g) + q == at - (LAST_Z if g == LAST else 0):
                return g, *divmod(c, len(tasks) // 2)
    return None


def post_start(w, p):
    if w == LAST:
        return LAST_PAIRS[1 + p]
    return LAST_PAIRS[0] if (w, p) == (LAST - 1, 1) else PAIR[p]


def due_post(s, q, *tasks):
    return [(w, p, c) for w in (s - 2, s - 1, s) if 0 <= w < UNITS for p in range(2) for c, at in enumerate(tasks)
            if QS * (s - 1 - w) + q == post_start(w, p) + at]


def state_of(g, j):
    if g == LAST:
        half, j = divmod(j, QS // 2)
        return j // 2, 2 * half + j % 2
    return divmod(j, LT)


def shared(g, j):
    return g != LAST and j // LT in SHARED


def shared_sums(g, j):
    if g == LAST:
        return LT * len(SHARED) * g
    return LT * (len(SHARED) * g + sum(m < j // LT for m in SHARED)) + (j % LT + 1 if shared(g, j) else 0)


def own_sums(g, j):
    return QS * g + j + 1 - shared_sums(g, j)


def last_scan(q):
    half, r = divmod(q, QS // 2)
    return half, r // 2, 2 * (r % 2), q // 2 % 2 * HL


def build(nc, x_d, xT_d, winT_d, convw_d, convb_d, xpT_d, dtT_d, dtb_d, alog_d, dskip_d, woT_d, w1_d, b1_d, w2_d,
          b2_d, out_d):
    bscr_d = nc.dram_tensor("b_rows", [UNITS, NS, L], F32, kind="Internal").ap()
    x_rows = x_d.rearrange("b (h q t p) m -> (b h) q p t m", h=SEQ // L, t=2, p=P)
    out_rows = out_d.rearrange("b (h q t p) m -> (b h) q p t m", h=SEQ // L, t=2, p=P)
    xT_cols = xT_d.rearrange("(c p) l -> p c l", p=P)

    ctx = ExitStack()
    with ctx:
        def sb(name, shape):
            return ctx.enter_context(nc.sbuf_tensor(name, shape, F32))

        def ps(name, shape):
            return ctx.enter_context(nc.psum_tensor(name, shape, F32))

        def sem(name):
            return ctx.enter_context(nc.semaphore(name))

        winT = sb("winT", [P, MT, 2 * DI])
        xpT = sb("xpT", [P, KT, XR])
        dtT = sb("dtT", [RK + 1, DI])
        woT = sb("woT", [P, KT, DM])
        w1 = sb("w1", [P, MT, FW])
        w2 = sb("w2", [P, WT, DM])
        b1 = sb("b1", [P, WT])
        b2 = sb("b2", [1, DM])
        convw = sb("convw", [P, KT, TAPS])
        convb = sb("convb", [P, KT])
        A = sb("A", [P, KT, NS])
        dskip = sb("dskip", [P, KT])
        ident = sb("ident", [P, P])
        diagD = sb("diagD", [P, KT, P])
        diagW = sb("diagW", [P, len(PE_TILES), TAPS, P])
        one = sb("one", [P, 1])
        mhalf = sb("mhalf", [P, 2])
        ln1 = sb("ln1", [P, 1])
        xT = sb("xT", [P, MT, L])
        xs = sb("xs", [P, KT, HALO + L])
        cv = sb("cv", [P, 2, L])
        sg = sb("sg", [P, 2, L])
        u = sb("u", [P, KT, L])
        xd = sb("xd", [XR, L])
        dtl = sb("dtl", [RK + 1, L])
        sp_t = sb("sp_t", [P, KT, L])
        sp_w = sb("sp_w", [P, 2, L])
        delta = sb("delta", [P, 2, KT, L])
        du = sb("du", [P, 2, KT, L])
        ct = sb("ct", [P, 2, LT, NS])
        bbc = sb("bbc", [P, B_RING, L])
        dbu = sb("dbu", [P, DB_RING, L])
        h = sb("h", [P, H_RING, KT, L])
        state = sb("state", [P, QS])
        acc = sb("acc", [P, 2, LT, DI])
        prod = sb("prod", [P, T_RING, DI])
        zg = sb("zg", [P, 2, KT, PW])
        xTz = sb("xTz", [P, MT, PW])
        xres = sb("xres", [P, 2, 2, DM])
        x1_all = sb("x1", [P, 2, DM])
        x1T_all = sb("x1T", [P, MT, PW])
        hid_all = sb("hid", [P, WT, PW])
        y2 = sb("y2", [P, 2, 2, DM])
        stats = sb("stats", [P, 2, 6])
        mv1 = sb("mv1", [P, 2, 2, 2])
        nm1 = sb("nm1", [P, 2, 2])
        rs1 = sb("rs1", [P, 2, 2])
        mv2 = sb("mv2", [P, 2, 2, 2])
        nm2 = sb("nm2", [P, 2, 2])
        rs2 = sb("rs2", [P, 2, 2])

        dA = [ps(f"dA{i}", [P, L]) for i in range(2)]
        hT = [ps(f"hT{i}", [P, DI]) for i in range(2)]
        pp = ps("pp", [P, 2, L])
        po_all = ps("po", [P, 2, 512])

        s_load = sem("s_load")
        s_load2 = sem("s_load2")
        s_load3 = sem("s_load3")
        s_const = sem("s_const")
        s_a = sem("s_a")
        s_chain = sem("s_chain")
        s_ach = sem("s_ach")
        s_xt = sem("s_xt")
        s_x = sem("s_x")
        s_halo = sem("s_halo")
        s_xs = sem("s_xs")
        s_cp = sem("s_cp")
        s_cv = [sem(f"s_cv{c}") for c in range(KT)]
        s_c = sem("s_c")
        s_s = sem("s_s")
        s_u = sem("s_u")
        s_xd = sem("s_xd")
        s_xdc = sem("s_xdc")
        s_bs = sem("s_bs")
        s_ctp = sem("s_ctp")
        s_ct = sem("s_ct")
        s_dt = sem("s_dt")
        s_sp = sem("s_sp")
        s_spv = sem("s_spv")
        s_delta = sem("s_delta")
        s_du = sem("s_du")
        s_udp = sem("s_udp")
        s_ud = sem("s_ud")
        s_b = [sem(f"s_b{i}") for i in range(B_RING)]
        s_da = sem("s_da")
        s_db = sem("s_db")
        s_scan = sem("s_scan")
        s_save = sem("s_save")
        s_ht = sem("s_ht")
        s_acc = sem("s_acc")
        s_prod = sem("s_prod")
        s_shared = sem("s_shared")
        s_xz = [sem(f"s_xz{i}") for i in range(2)]
        s_xr = [sem(f"s_xr{i}") for i in range(2)]
        s_z = sem("s_z")
        s_ln = sem("s_ln")
        s_half = sem("s_half")
        s_var1 = [sem(f"s_var1{p}") for p in range(2)]
        s_rs1 = [sem(f"s_rs1{p}") for p in range(2)]
        s_var2 = [sem(f"s_var2{p}") for p in range(2)]
        s_rs2 = [sem(f"s_rs2{p}") for p in range(2)]
        s_zs = sem("s_zs")
        s_zg = sem("s_zg")
        s_yt = [sem(f"s_yt{p}") for p in range(2)]
        s_yg = [sem(f"s_yg{p}") for p in range(2)]
        s_o = [sem(f"s_o{p}") for p in range(2)]
        s_r1 = [sem(f"s_r1{p}") for p in range(2)]
        s_x1 = [sem(f"s_x1{p}") for p in range(2)]
        s_tp = [sem(f"s_tp{p}") for p in range(2)]
        s_x1T = [sem(f"s_x1T{p}") for p in range(2)]
        s_f1 = [sem(f"s_f1{p}") for p in range(2)]
        s_hid = [sem(f"s_hid{p}") for p in range(2)]
        s_f2 = [sem(f"s_f2{p}") for p in range(2)]
        s_r2 = [sem(f"s_r2{p}") for p in range(2)]
        s_y2 = [sem(f"s_y2{p}") for p in range(2)]
        s_out = [sem(f"s_out{i}") for i in range(2)]

        def bank(v, c):
            return po_all[:, c - 2, :] if v == 0 and c >= 2 else pp[:, c % 2, :]

        def conv(v, c):
            return delta[:, 1, c, :] if v == 0 else cv[:, c % 2, :]

        def buffers(w, p):
            if p and w >= LAST - 1:
                return (pp, *[sp_t[:, c, :].rearrange("p (t m) -> p t m", t=2) for c in range(2)],
                        u[:].rearrange("p k (a l) -> p (k a) l", a=2))
            return po_all, x1_all[:], x1T_all[:], hid_all[:]

        def pair_before(w, p):
            if (w, p) == (LAST - 1, 1):
                return None
            if w == LAST:
                return p, LAST
            return (0, w + 1) if p else (1, w) if w else None

        def gate(w, p):
            if w == LAST:
                return delta[:, 1 - LAST % 2, 2 * p:2 * p + 2, :].rearrange("p a (b l) -> p (a b) l", b=2)
            return zg[:, p]

        def has_main(s):
            return 0 <= s < UNITS

        def has_prep(s):
            return s + 1 < UNITS

        LOADS, LOADS2, LOADS3 = 16 * 3, 16 * 5, 16 * 6
        block = ctx.enter_context(nc.Block())

        @block.sync
        def _(sp):
            sp.dma_start(xT[:], xT_cols[:, :, 0:L]).then_inc(s_xt, 16)
            sp.dma_start(winT[:, :, 0:DI], winT_d.rearrange("(c p) n -> p c n", p=P)[:, :, 0:DI]).then_inc(s_load, 16)
            sp.dma_start(convw[:], convw_d.rearrange("(k p) a t -> p k (a t)", p=P)).then_inc(s_load, 16)
            sp.dma_start(convb[:], convb_d).then_inc(s_load, 16)
            sp.dma_start(dskip[:], dskip_d).then_inc(s_load2, 16)
            sp.dma_start(A[:], alog_d.rearrange("(k p) n -> p k n", p=P)).then_inc(s_load2, 16)
            sp.dma_start(xpT[:], xpT_d.rearrange("(k p) n -> p k n", p=P)).then_inc(s_load2, 16)
            sp.dma_start(dtT[0:RK, :], dtT_d).then_inc(s_load2, 16)
            sp.dma_start(dtT[RK:RK + 1, :], dtb_d.rearrange("(a n) -> a n", a=1)).then_inc(s_load2, 16)
            sp.dma_start(winT[:, :, DI:], winT_d.rearrange("(c p) n -> p c n", p=P)[:, :, DI:]).then_inc(s_load3, 16)
            sp.dma_start(woT[:], woT_d.rearrange("(k p) n -> p k n", p=P)).then_inc(s_load3, 16)
            sp.dma_start(w1[:], w1_d.rearrange("(c p) n -> p c n", p=P)).then_inc(s_load3, 16)
            sp.dma_start(b1[:], b1_d).then_inc(s_load3, 16)
            sp.dma_start(w2[:], w2_d.rearrange("(w p) n -> p w n", p=P)).then_inc(s_load3, 16)
            sp.dma_start(b2[:], b2_d.rearrange("(a n) -> a n", a=1)).then_inc(s_load3, 16)

            def load_b(t):
                g, n = divmod(t, NS)
                if t >= B_RING:
                    sp.wait_ge(s_db, KT * (t - B_RING + 1))
                if n == 0:
                    sp.wait_ge(s_bs, 16 * (g + 1))
                if g == LAST:
                    half, n = divmod(2 * n, NS)
                    sp.dma_start(bbc[:, t % B_RING, :].rearrange("p (a l) -> p a l", a=2),
                                 bscr_d[g, n:n + 2, half * HL:(half + 1) * HL].unsqueeze(0).broadcast_to(
                                     [P, 2, HL])).then_inc(s_b[t % B_RING], 16)
                    return
                sp.dma_start(bbc[:, t % B_RING, :], bscr_d[g, n:n + 1, :].broadcast_to([P, L])).then_inc(
                    s_b[t % B_RING], 16)

            for s in range(-1, UNITS + 2):
                for q in range(QS):
                    n, k = divmod(q, KT)
                    if (task := due_prep(s, q, X_PE[-1] + 2)) and task[0] + 1 < UNITS:
                        v = task[0]
                        sp.wait_ge(s_x, KT * (v + 1))
                        sp.dma_start(xT[:], xT_cols[:, :, (v + 1) * L:(v + 2) * L]).then_inc(s_xt, 16)
                    if task := due_prep(s, q, XD_ACT + 1):
                        v = task[0]
                        sp.wait_ge(s_xdc, 2 * (v + 1))
                        sp.dma_start(bscr_d[v], xd[RK:RK + NS, :]).then_inc(s_bs, 16)
                    ahead = NS * s + n + B_RING - 1
                    if k == 0 and 0 <= ahead < UNITS * NS and s < UNITS:
                        load_b(ahead)
                    if task := due_gate(s, q, *XZ_SP):
                        g, p, _ = task
                        if g or p:
                            sp.wait_ge(s_z, 4 * g + 2 * p)
                        at = g * L + p * PW
                        sp.dma_start(xTz[:], xT_cols[:, :, at:at + PW]).then_inc(s_xz[p], 16)
                    for p in range(2):
                        if has_main(s) and q == XR_SP[p] - (LAST_XR if (s, p) == (LAST, 0) else 0):
                            if s >= 1:
                                sp.wait_ge(s_r1[p], s)
                            sp.dma_start(xres[:, p], x_rows[s, p]).then_inc(s_xr[p], 16)
                    for w, p, _ in due_post(s, q, OUT_SP):
                        sp.wait_ge(s_y2[p], 2 * (w + 1))
                        sp.dma_start(out_rows[w, p], y2[:, p]).then_inc(s_out[p], 16)
            for p in range(2):
                sp.wait_ge(s_out[p], 16 * UNITS)

        @block.gpsimd
        def _(gp):
            nc.gpsimd.memset(ident[:], 0.0).then_inc(s_a, 1)
            nc.gpsimd.memset(dtl[:], 2.0).then_inc(s_const, 1)
            nc.gpsimd.memset(one[:], 1.0).then_inc(s_const, 1)
            nc.gpsimd.memset(mhalf[:], -0.5).then_inc(s_const, 1)
            gp.wait_ge(s_a, 1)
            nc.gpsimd.affine_select(out=ident[:], in_=ident[:], compare_op=ALU.not_equal, fill=1.0, base=0,
                                    pattern=[[-1, P]], channel_multiplier=1).then_inc(s_const, 1)
            gp.wait_ge(s_const, 4)
            gp.wait_ge(s_half, 2)
            for i, c in enumerate(PE_TILES):
                nc.gpsimd.tensor_tensor(diagW[:, i], ident[:].unsqueeze(1).broadcast_to([P, TAPS, P]),
                                        convw[:, c, :].unsqueeze(2).broadcast_to([P, TAPS, P]),
                                        ALU.mult).then_inc(s_const, 1)
            gp.wait_ge(s_load2, LOADS2)
            nc.gpsimd.tensor_tensor(diagD[:], ident[:].unsqueeze(1).broadcast_to([P, KT, P]),
                                    dskip[:].unsqueeze(2).broadcast_to([P, KT, P]), ALU.mult).then_inc(s_const, 1)
            for s in range(-1, UNITS + 2):
                for q in range(QS):
                    n, k = divmod(q, KT)
                    if has_main(s):
                        i, t = QS * s + q, NS * s + n
                        if k == 0:
                            gp.wait_ge(s_b[t % B_RING], 16 * (t // B_RING + 1))
                        if n == 0:
                            gp.wait_ge(s_du, KT * s + (min(KT, 2 * k + 2) if s == LAST else k + 1))
                        if i >= DB_RING:
                            gp.wait_ge(s_scan, i - DB_RING + 1)
                        if s == LAST:
                            half, _, c, at = last_scan(q)
                            b_row = bbc[:, t % B_RING, at:at + HL]
                            nc.gpsimd.tensor_tensor(dbu[:, i % DB_RING, :].rearrange("p (a l) -> p a l", a=2),
                                                    du[:, s % 2, c:c + 2, half * HL:(half + 1) * HL],
                                                    b_row.unsqueeze(1).broadcast_to([P, 2, HL]),
                                                    ALU.mult).then_inc(s_db, 1)
                        else:
                            nc.gpsimd.tensor_tensor(dbu[:, i % DB_RING, :], du[:, s % 2, k, :], bbc[:, t % B_RING, :],
                                                    ALU.mult).then_inc(s_db, 1)
                    g, j = divmod(QS * s + q - KT - SHARED_GP, QS)
                    if has_main(g) and shared(g, j):
                        t = j % LT
                        i = shared_sums(g, j)
                        gp.wait_ge(s_prod, i)
                        gp.wait_ge(s_acc, own_sums(g, j - LT))
                        nc.gpsimd.tensor_tensor(acc[:, g % 2, t, :], acc[:, g % 2, t, :], prod[:, (i - 1) % T_RING, :],
                                                ALU.add).then_inc(s_shared, 1)
                    if (task := due_prep(s, q, *DU_GP)) and task[0]:
                        v, c = task
                        gp.wait_ge(s_delta, KT * v + c + 1)
                        nc.gpsimd.tensor_tensor(du[:, v % 2, c, :], delta[:, v % 2, c, :], u[:, c, :],
                                                ALU.mult).then_inc(s_du, 1)
                    for w, p, _ in due_post(s, q, POW1_GP):
                        gp.wait_ge(s_var1[p], w + 1)
                        nc.gpsimd.tensor_tensor(rs1[:, p], rs1[:, p], mhalf[:], ALU.pow).then_inc(s_rs1[p], 1)
                    for w, p, _ in due_post(s, q, POW2_GP):
                        gp.wait_ge(s_var2[p], w + 1)
                        nc.gpsimd.tensor_tensor(rs2[:, p], rs2[:, p], mhalf[:], ALU.pow).then_inc(s_rs2[p], 1)

        @block.scalar
        def _(act):
            own = [0]

            def link(ins):
                own[0] += 1
                ins.then_inc(s_ach, 1)
                act.wait_ge(s_ach, own[0])

            def normalize(out, src, nm, rs, s_out):
                nc.scalar.activation(nm[:, 0:1], nm[:, 0:1], ACT.Copy, scale=rs[:, 0:1])
                link(nc.scalar.activation(nm[:, 1:2], nm[:, 1:2], ACT.Copy, scale=rs[:, 1:2]))
                for t in range(2):
                    nc.scalar.activation(out[:, t, :], src[:, t, :], ACT.Identity, bias=nm[:, t:t + 1],
                                         scale=rs[:, t:t + 1]).then_inc(s_out, 1)

            act.wait_ge(s_const, 4)
            nc.scalar.activation(ln1[:], one[:], ACT.Tanh)
            act.wait_ge(s_half, 2)
            for s in range(-1, UNITS + 2):
                for q in range(QS):
                    n, k = divmod(q, KT)
                    if has_main(s):
                        i = QS * s + q
                        if n == 0:
                            act.wait_ge(s_delta, KT * s + (min(KT, 2 * k + 2) if s == LAST else k + 1))
                        if i >= 2:
                            act.wait_ge(s_scan, i - 1)
                        if s == LAST:
                            half, m, c, _ = last_scan(q)
                            for b in range(2):
                                step = nc.scalar.activation(dA[i % 2][:, b * HL:(b + 1) * HL],
                                                            delta[:, s % 2, c + b, half * HL:(half + 1) * HL], ACT.Exp,
                                                            scale=A[:, c + b, m:m + 1])
                            step.then_inc(s_da, 1)
                        else:
                            nc.scalar.activation(dA[i % 2][:, :], delta[:, s % 2, k, :], ACT.Exp,
                                                 scale=A[:, k, n:n + 1]).then_inc(s_da, 1)
                    g, j = divmod(QS * s + q - KT - SHARED_ACT, QS)
                    if has_main(g) and shared(g, j):
                        m, t = state_of(g, j)
                        i = shared_sums(g, j)
                        act.wait_ge(s_ht, QS * g + j + 1)
                        if i > T_RING:
                            act.wait_ge(s_shared, i - T_RING)
                        if m == SHARED[0] and t == 0:
                            act.wait_ge(s_ct, g + 1)
                        nc.scalar.activation(prod[:, (i - 1) % T_RING, :], hT[t % 2][:, :], ACT.Copy,
                                             scale=ct[:, g % 2, t, m:m + 1]).then_inc(s_prod, 1)
                    if task := due_prep(s, q, *X_ACT, first=FIRST_X_ACT):
                        v, c = task
                        act.wait_ge(s_x, KT * v + c + 1)
                        act.wait_ge(s_halo, v + 1)
                        if v:
                            act.wait_ge(s_u, KT * (v - 1) + c + 1)
                        nc.scalar.activation(xs[:, c, HALO:], bank(v, c), ACT.Copy).then_inc(s_xs, 1)
                        if c in VE_TILES:
                            if v:
                                act.wait_ge(s_u, KT * v + c - 1)
                            nc.scalar.activation(conv(v, c), bank(v, c), ACT.Identity,
                                                 bias=convb[:, c:c + 1],
                                                 scale=convw[:, c, HALO:TAPS]).then_inc(s_cv[c], 1)
                    if task := due_prep(s, q, *CV_ACT, first=FIRST_CV_ACT):
                        v, c = task[0], PE_TILES[task[1]]
                        act.wait_ge(s_cp, len(PE_TILES) * v + task[1] + 1)
                        if v:
                            act.wait_ge(s_u, KT * v + c - 1)
                        nc.scalar.activation(conv(v, c), bank(v, c), ACT.Identity,
                                             bias=convb[:, c:c + 1]).then_inc(s_cv[c], 1)
                    if task := due_prep(s, q, *X_TANH, first=FIRST_X_TANH):
                        v, c = task
                        if c in VE_TILES:
                            act.wait_ge(s_c, len(VE_TILES) * v + VE_TILES.index(c) + 1)
                        else:
                            act.wait_ge(s_cv[c], v + 1)
                        if KT * v + c >= 2:
                            act.wait_ge(s_u, KT * v + c - 1)
                        nc.scalar.activation(sg[:, c % 2, :], conv(v, c), ACT.Tanh).then_inc(s_s, 1)
                    if s == -1 and q == SETUP:
                        act.wait_ge(s_load2, LOADS2)
                        link(nc.scalar.activation(A[:], A[:], ACT.Exp))
                        link(nc.scalar.activation(A[:], A[:], ACT.Copy, scale=-1.0))
                    if task := due_prep(s, q, XD_ACT):
                        v = task[0]
                        act.wait_ge(s_xd, v + 1)
                        if v >= 1:
                            act.wait_ge(s_bs, 16 * v)
                        nc.scalar.activation(xd[:, :], pp[0:XR, 0, :], ACT.Copy).then_inc(s_xdc, 1)
                        nc.scalar.activation(dtl[0:RK, :], pp[0:RK, 0, :], ACT.Copy).then_inc(s_xdc, 1)
                    if task := due_prep(s, q, CT_ACT):
                        v = task[0]
                        act.wait_ge(s_ctp, v + 1)
                        nc.scalar.activation(
                            ct[:, v % 2], pp[:, 1, 0:LT * XR].rearrange("p (t r) -> p t r", r=XR)[:, :, RK + NS:XR],
                            ACT.Copy).then_inc(s_ct, 1)
                    if task := due_prep(s, q, *DT_ACT, first=FIRST_DT_ACT):
                        v, c = task
                        m = KT * v + c
                        act.wait_ge(s_dt, m + 1)
                        if v:
                            act.wait_ge(s_delta, KT * v)
                        if m >= 2:
                            act.wait_ge(s_spv, 2 * (m - 1))
                        link(nc.scalar.activation(sp_t[:, c, :], bank(v, c), ACT.Abs))
                        link(nc.scalar.activation(sp_t[:, c, :], sp_t[:, c, :], ACT.Exp, scale=-1.0))
                        nc.scalar.activation(sp_w[:, c % 2, :], sp_t[:, c, :], ACT.Identity,
                                             bias=one[:, 0:1]).then_inc(s_sp, 1)
                    if task := due_prep(s, q, LN_ACT):
                        v = task[0]
                        if v == 0:
                            link(nc.scalar.activation(ln1[:], one[:], ACT.Ln))
                        act.wait_ge(s_spv, 2 * KT * (v + 1))
                        nc.scalar.activation(sp_t[:], sp_t[:], ACT.Ln, bias=one[:, 0:1]).then_inc(s_ln, 1)
                    if task := due_prep(s, q, *UD_ACT):
                        v, t = task
                        act.wait_ge(s_udp, LT * v + t + 1)
                        if v >= 2:
                            act.wait_ge(s_yt[1], v - 1)
                        nc.scalar.activation(acc[:, v % 2, t, :], pp[:, t % 2, :], ACT.Copy).then_inc(s_ud, 1)
                    if task := due_gate(s, q, *Z_ACT):
                        g, p, b = task
                        act.wait_ge(s_z, 4 * g + 2 * p + b + 1)
                        if 0 < g < LAST:
                            act.wait_ge(s_o[p], g)
                        nc.scalar.activation(gate(g, p)[:, 2 * b:2 * b + 2, :], pp[:, b, :].rearrange(
                            "p (k l) -> p k l", k=2), ACT.Tanh, scale=0.5).then_inc(s_zs, 1)
                    for w, p, _ in due_post(s, q, N1_ACT):
                        x1 = buffers(w, p)[1]
                        act.wait_ge(s_rs1[p], w + 1)
                        normalize(x1, x1, nm1[:, p], rs1[:, p], s_x1[p])
                    for w, p, _ in due_post(s, q, N2_ACT):
                        act.wait_ge(s_rs2[p], w + 1)
                        if w >= 1:
                            act.wait_ge(s_out[p], 16 * w)
                        normalize(y2[:, p], buffers(w, p)[1], nm2[:, p], rs2[:, p], s_y2[p])
                    for w, p, _ in due_post(s, q, T_ACT):
                        act.wait_ge(s_tp[p], w + 1)
                        po, _, x1T, _ = buffers(w, p)
                        nc.scalar.activation(x1T.rearrange("p c l -> p (c l)"), po[:, 1, :],
                                             ACT.Copy).then_inc(s_x1T[p], 1)
                    for w, p, f in due_post(s, q, *F1_ACT):
                        act.wait_ge(s_f1[p], 4 * w + f + 1)
                        po, _, _, hid = buffers(w, p)
                        for a in range(2):
                            nc.scalar.activation(hid[:, 2 * f + a, :], po[:, f % 2, a * PW:(a + 1) * PW], ACT.Relu,
                                                 bias=b1[:, 2 * f + a:2 * f + a + 1]).then_inc(s_hid[p], 1)

        @block.vector
        def _(dve):
            own = [0]

            def link(ins):
                own[0] += 1
                ins.then_inc(s_chain, 1)
                dve.wait_ge(s_chain, own[0])

            def accumulate(g, j):
                n, t = state_of(g, j)
                dve.wait_ge(s_ht, QS * g + j + 1)
                before = j - (2 if g == LAST else LT)
                if n == 0:
                    dve.wait_ge(s_ud, LT * g + t + 1)
                    dve.wait_ge(s_ct, g + 1)
                elif shared(g, before):
                    dve.wait_ge(s_shared, shared_sums(g, before))
                else:
                    dve.wait_ge(s_acc, own_sums(g, before))
                nc.vector.scalar_tensor_tensor(out=acc[:, g % 2, t, :], in0=hT[t % 2][:, :],
                                               scalar=ct[:, g % 2, t, n:n + 1], in1=acc[:, g % 2, t, :],
                                               op0=ALU.mult, op1=ALU.add).then_inc(s_acc, 1)

            def row_moments(src, mv, nm, rs, s_var):
                nc.vector.bn_stats(stats[:, 0, :], src[:, 0, :])
                link(nc.vector.bn_stats(stats[:, 1, :], src[:, 1, :]))
                nc.vector.bn_aggr(mv[:, 0, :], stats[:, 0, :])
                link(nc.vector.bn_aggr(mv[:, 1, :], stats[:, 1, :]))
                nc.vector.tensor_scalar(nm, mv[:, :, 0], -1.0, None, ALU.mult)
                nc.vector.tensor_scalar(rs, mv[:, :, 1], EPS, None, ALU.add).then_inc(s_var, 1)

            dve.wait_ge(s_load, LOADS)
            nc.vector.tensor_scalar(convw[:], convw[:], 0.5, None, ALU.mult).then_inc(s_half, 1)
            nc.vector.tensor_scalar(convb[:], convb[:], 0.5, None, ALU.mult).then_inc(s_half, 1)
            dve.wait_ge(s_half, 2)
            for s in range(-1, UNITS + 2):
                v = s + 1
                if has_prep(s):
                    if v:
                        for c in PE_TILES:
                            dve.wait_ge(s_cv[c], v)
                    if v % 2 == 0:
                        nc.vector.memset(xs[:, :, 0:HALO], 0.0).then_inc(s_halo, 1)
                    else:
                        dve.wait_ge(s_xs, KT * v)
                        nc.vector.tensor_copy(xs[:, :, 0:HALO], xs[:, :, L:L + HALO]).then_inc(s_halo, 1)
                for q in range(QS):
                    n, k = divmod(q, KT)
                    if has_main(s):
                        i = QS * s + q
                        dve.wait_ge(s_da, i + 1)
                        dve.wait_ge(s_db, i + 1)
                        state_no = NS * s + n
                        if state_no >= H_RING:
                            dve.wait_ge(s_ht, LT * (state_no - H_RING + 1))
                        first = s % 2 == 0
                        if s == LAST:
                            half, m, c, at = last_scan(q)
                            dve.wait_ge(s_save, NS * (UNITS // 2 if half else s // 2) + m + 1)
                            for b in range(2):
                                step = nc.vector.tensor_tensor_scan(
                                    h[:, state_no % H_RING, c + b, at:at + HL], dA[i % 2][:, b * HL:(b + 1) * HL],
                                    dbu[:, i % DB_RING, b * HL:(b + 1) * HL],
                                    state[:, KT * m + c + b:KT * m + c + b + 1],
                                    ALU.mult, ALU.add)
                            step.then_inc(s_scan, 1)
                        else:
                            if not first:
                                dve.wait_ge(s_save, NS * (s // 2) + n + 1)
                            nc.vector.tensor_tensor_scan(
                                h[:, state_no % H_RING, k, :], dA[i % 2][:, :], dbu[:, i % DB_RING, :],
                                0.0 if first else state[:, KT * n + k:KT * n + k + 1],
                                ALU.mult, ALU.add).then_inc(s_scan, 1)
                    m, g = (n - 1, s) if n else (NS - 1, s - 1)
                    if has_main(g):
                        if k == 0 and g % 2 == 0:
                            dve.wait_ge(s_scan, QS * g + KT * (m + 1))
                            nc.vector.tensor_copy(state[:, KT * m:KT * (m + 1)].unsqueeze(2),
                                                  h[:, (NS * g + m) % H_RING, :, L - 1:L]).then_inc(s_save, 1)
                    if s == LAST and q % 2 == 0 and 0 < q <= QS // 2:
                        _, m, _, at = last_scan(q - 2)
                        dve.wait_ge(s_scan, QS * s + q)
                        nc.vector.tensor_copy(state[:, KT * m:KT * (m + 1)].unsqueeze(2),
                                              h[:, (NS * s + (q - 2) // KT) % H_RING, :, at + HL - 1:at + HL]).then_inc(
                            s_save, 1)
                    g, j = divmod(QS * s + q - KT - ACC_DVE, QS)
                    if has_main(g) and not shared(g, j):
                        accumulate(g, j)
                    if s == 0 and q == SETUP:
                        dve.wait_ge(s_load3, LOADS3)
                        nc.vector.tensor_scalar(woT[:], woT[:], 0.5, None, ALU.mult).then_inc(s_half, 1)
                    if task := due_prep(s, q, *X_DVE, first=FIRST_X_DVE):
                        v, c = task[0], VE_TILES[task[1]]
                        dve.wait_ge(s_cv[c], v + 1)
                        dve.wait_ge(s_halo, v + 1)
                        for j in range(1, TAPS):
                            tap = (nc.vector.scalar_tensor_tensor(
                                out=conv(v, c), in0=xs[:, c, HALO - j:HALO - j + L],
                                scalar=convw[:, c, HALO - j:TAPS - j], in1=conv(v, c),
                                op0=ALU.mult, op1=ALU.add))
                            if j < HALO:
                                link(tap)
                        tap.then_inc(s_c, 1)
                    if task := due_prep(s, q, *U_DVE, first=FIRST_U_DVE):
                        v, c = task
                        dve.wait_ge(s_s, KT * v + c + 1)
                        if v:
                            dve.wait_ge(s_udp, LT * v)
                        nc.vector.scalar_tensor_tensor(out=u[:, c, :], in0=sg[:, c % 2, :], scalar=1.0,
                                                       in1=conv(v, c), op0=ALU.add,
                                                       op1=ALU.mult).then_inc(s_u, 1)
                    if task := due_prep(s, q, *DT_DVE, first=FIRST_DT_DVE):
                        v, c = task
                        m1 = KT * v + c
                        dve.wait_ge(s_sp, m1 + 1)
                        nc.vector.scalar_tensor_tensor(out=sp_w[:, c % 2, :], in0=sp_w[:, c % 2, :], scalar=1.0,
                                                       in1=sp_t[:, c, :], op0=ALU.subtract,
                                                       op1=ALU.subtract).then_inc(s_spv, 1)
                        dve.wait_ge(s_spv, 2 * m1 + 1)
                        nc.vector.scalar_tensor_tensor(out=delta[:, v % 2, c, :], in0=bank(v, c), scalar=0.0,
                                                       in1=sp_w[:, c % 2, :], op0=ALU.max,
                                                       op1=ALU.subtract).then_inc(s_spv, 1)
                    if task := due_prep(s, q, *DELTA_DVE):
                        v, c = task
                        dve.wait_ge(s_ln, v + 1)
                        dve.wait_ge(s_spv, 2 * (KT * v + c + 1))
                        nc.vector.scalar_tensor_tensor(out=delta[:, v % 2, c, :], in0=sp_t[:, c, :], scalar=ln1[:, 0:1],
                                                       in1=delta[:, v % 2, c, :], op0=ALU.subtract,
                                                       op1=ALU.add).then_inc(s_delta, 1)
                        if v == 0:
                            dve.wait_ge(s_delta, c + 1)
                            nc.vector.tensor_tensor(du[:, 0, c, :], delta[:, 0, c, :], u[:, c, :],
                                                    ALU.mult).then_inc(s_du, 1)
                    if task := due_gate(s, q, *Z_DVE):
                        g, p, b = task
                        dve.wait_ge(s_zs, 4 * g + 2 * p + b + 1)
                        z = gate(g, p)[:, 2 * b:2 * b + 2, :]
                        nc.vector.scalar_tensor_tensor(out=z, in0=z, scalar=1.0, in1=pp[:, b, :].rearrange(
                            "p (k l) -> p k l", k=2), op0=ALU.add,
                                                       op1=ALU.mult).then_inc(s_zg, 1)
                    for w, p, _ in due_post(s, q, YG_DVE):
                        po = buffers(w, p)[0]
                        dve.wait_ge(s_yt[p], w + 1)
                        dve.wait_ge(s_zg, 2 * (2 * w + p + 1))
                        nc.vector.tensor_tensor(gate(w, p), po[:, :, :].rearrange("p a (k l) -> p (a k) l", k=2),
                                                gate(w, p), ALU.mult).then_inc(s_yg[p], 1)
                    for w, p, _ in due_post(s, q, R1_DVE):
                        po, x1 = buffers(w, p)[:2]
                        dve.wait_ge(s_o[p], w + 1)
                        if before := pair_before(w, p):
                            dve.wait_ge(s_y2[before[0]], 2 * before[1])
                        dve.wait_ge(s_xr[p], 16 * (w + 1))
                        nc.vector.tensor_tensor(x1.rearrange("p t m -> p (t m)"), po[:, 0, :],
                                                xres[:, p].rearrange("p t m -> p (t m)"), ALU.add).then_inc(s_r1[p], 1)
                        dve.wait_ge(s_r1[p], w + 1)
                        row_moments(x1, mv1[:, p], nm1[:, p], rs1[:, p], s_var1[p])
                    for w, p, _ in due_post(s, q, R2_DVE):
                        po, x1 = buffers(w, p)[:2]
                        dve.wait_ge(s_f2[p], w + 1)
                        nc.vector.tensor_tensor(x1.rearrange("p t m -> p (t m)"), po[:, 0, :],
                                                x1.rearrange("p t m -> p (t m)"), ALU.add).then_inc(s_r2[p], 1)
                        dve.wait_ge(s_r2[p], w + 1)
                        row_moments(x1, mv2[:, p], nm2[:, p], rs2[:, p], s_var2[p])

        @block.tensor
        def _(pe):
            def mm(out, lhsT, rhs, start=True, stop=True):
                return nc.tensor.matmul(out, lhsT, rhs, start=start, stop=stop)

            pe.wait_ge(s_load, LOADS)
            for s in range(-1, UNITS + 2):
                for q in range(QS):
                    n, t = divmod(q, LT)
                    g, m = (s, n - 1) if n else (s - 1, NS - 1)
                    if has_main(g):
                        j = QS * g + LT * m + t
                        pe.wait_ge(s_scan, QS * g + KT * (m + 1))
                        if j >= 2:
                            before = divmod(j - 2, QS)
                            if shared(*before):
                                pe.wait_ge(s_prod, shared_sums(*before))
                            else:
                                pe.wait_ge(s_acc, own_sums(*before))
                        for c in range(KT):
                            last = nc.tensor.transpose(hT[t % 2][:, c * P:(c + 1) * P],
                                                       h[:, (NS * g + m) % H_RING, c, t * P:(t + 1) * P], ident[:])
                        last.then_inc(s_ht, 1)
                    if task := due_prep(s, q, *X_PE, first=FIRST_X_PE):
                        v, c = task
                        if c == 0:
                            pe.wait_ge(s_xt, 16 * (v + 1))
                        if v and c >= 2:
                            pe.wait_ge(s_cv[c - 2], v + 1)
                        elif v:
                            pe.wait_ge(s_ud, LT * v - 1 + c)
                        for a in range(MT):
                            last = mm(bank(v, c), winT[:, a, c * P:(c + 1) * P], xT[:, a, :],
                                      a == 0, a == MT - 1)
                        last.then_inc(s_x, 1)
                    if task := due_prep(s, q, *CONV_PE, first=FIRST_CONV_PE):
                        v, i = task
                        c = PE_TILES[i]
                        pe.wait_ge(s_xs, KT * v + c + 1)
                        pe.wait_ge(s_halo, v + 1)
                        if v == 0:
                            pe.wait_ge(s_const, 4 + len(PE_TILES))
                        for j in range(TAPS):
                            last = mm(bank(v, c), diagW[:, i, j, :], xs[:, c, j:j + L], j == 0, j == TAPS - 1)
                        last.then_inc(s_cp, 1)
                    if task := due_prep(s, q, *XD_PE):
                        v, b = task
                        if b == 0:
                            for c in range(KT):
                                pe.wait_ge(s_cv[c], v + 1)
                        if v == 0:
                            pe.wait_ge(s_load2, LOADS2)
                            pe.wait_ge(s_const, 5 + len(PE_TILES))
                        pe.wait_ge(s_u, KT * v + 2 * (b + 1))
                        for c in (2 * b, 2 * b + 1):
                            last = mm(pp[0:XR, 0, :], xpT[:, c, :], u[:, c, :], c == 0, c == KT - 1)
                        if b:
                            last.then_inc(s_xd, 1)
                    if task := due_prep(s, q, CT_PE):
                        v = task[0]
                        pe.wait_ge(s_xdc, 2 * (v + 1))
                        for t in range(LT):
                            last = nc.tensor.transpose(pp[:, 1, t * XR:(t + 1) * XR], xd[:, t * P:(t + 1) * P],
                                                       ident[0:XR, 0:XR])
                        last.then_inc(s_ctp, 1)
                    if task := due_prep(s, q, *DT_PE, first=FIRST_DT_PE):
                        v, c = task
                        if c == 1:
                            pe.wait_ge(s_ct, v + 1)
                        if v and c >= 2:
                            pe.wait_ge(s_spv, 2 * (KT * v + c - 1))
                        mm(bank(v, c), dtT[:, c * P:(c + 1) * P], dtl[:, :]).then_inc(s_dt, 1)
                    if task := due_gate(s, q, *Z_PE):
                        g, p, b = task
                        if b == 0:
                            pe.wait_ge(s_xz[p], 16 * (g + 1))
                        if g == 0:
                            pe.wait_ge(s_load3, LOADS3)
                        if p:
                            pe.wait_ge(s_zg, 4 * g + b + 1)
                        elif g < LAST:
                            pe.wait_ge(s_spv, 2 * (KT * (g + 1) + 3 + b))
                        else:
                            pe.wait_ge(s_ud, LT * UNITS)
                        for c in (2 * b, 2 * b + 1):
                            for a in range(MT):
                                last = mm(pp[:, b, (c % 2) * PW:(c % 2 + 1) * PW],
                                          winT[:, a, DI + c * P:DI + (c + 1) * P], xTz[:, a, :],
                                          a == 0, a == MT - 1)
                        last.then_inc(s_z, 1)
                    if task := due_prep(s, q, *UD_PE):
                        v, t = task
                        if t >= 2:
                            pe.wait_ge(s_ud, LT * v + t - 1)
                        elif v:
                            pe.wait_ge(s_zg, 4 * (v - 1) + 3 + t)
                        else:
                            pe.wait_ge(s_spv, 2 * (KT * v + 3 + t))
                        for c in range(KT):
                            last = mm(pp[:, t % 2, c * P:(c + 1) * P], u[:, c, t * P:(t + 1) * P], diagD[:, c, :])
                        last.then_inc(s_udp, 1)
                    for w, p, _ in due_post(s, q, Y_PE):
                        po = buffers(w, p)[0]
                        done = (QS - 1 if p else QS // 2 - 1) if w == LAST else QS - LT + 2 * p + 1
                        pe.wait_ge(s_acc, own_sums(w, done))
                        pe.wait_ge(s_shared, shared_sums(w, done))
                        if before := pair_before(w, p):
                            pe.wait_ge(s_r2[before[0]], before[1])
                        elif w:
                            pe.wait_ge(s_zg, 4 * UNITS)
                        for c in range(KT):
                            for t in range(2):
                                last = nc.tensor.transpose(
                                    po[:, c // 2, (c % 2) * PW + t * P:(c % 2) * PW + (t + 1) * P],
                                    acc[:, w % 2, 2 * p + t, c * P:(c + 1) * P], ident[:])
                        last.then_inc(s_yt[p], 1)
                    for w, p, t in due_post(s, q, *O_PE):
                        po = buffers(w, p)[0]
                        pe.wait_ge(s_yg[p], w + 1)
                        pe.wait_ge(s_half, 3)
                        for c in range(KT):
                            last = mm(po[:, 0, t * DM:(t + 1) * DM], gate(w, p)[:, c, t * P:(t + 1) * P],
                                      woT[:, c, :], c == 0, c == KT - 1)
                        if t:
                            last.then_inc(s_o[p], 1)
                    for w, p, _ in due_post(s, q, T_PE):
                        po, x1 = buffers(w, p)[:2]
                        pe.wait_ge(s_x1[p], 2 * (w + 1))
                        for a in range(MT):
                            for t in range(2):
                                last = nc.tensor.transpose(po[:, 1, a * PW + t * P:a * PW + (t + 1) * P],
                                                           x1[:, t, a * P:(a + 1) * P], ident[:])
                        last.then_inc(s_tp[p], 1)
                    for w, p, f in due_post(s, q, *F1_PE):
                        po, _, x1T, _ = buffers(w, p)
                        if f < 2:
                            pe.wait_ge(s_x1T[p], w + 1)
                        else:
                            pe.wait_ge(s_hid[p], WT * w + 2 * (f - 1))
                        for a in range(2):
                            for c in range(MT):
                                at_w = (2 * f + a) * P
                                last = mm(po[:, f % 2, a * PW:(a + 1) * PW], w1[:, c, at_w:at_w + P],
                                          x1T[:, c, :], c == 0, c == MT - 1)
                        last.then_inc(s_f1[p], 1)
                    for w, p, b in due_post(s, q, *F2_PE):
                        t, b = divmod(b, 2)
                        po, _, _, hid = buffers(w, p)
                        pe.wait_ge(s_hid[p], WT * (w + 1) - (0 if t or b else 2))
                        for a in range(4 * b, 4 * b + 4):
                            last = mm(po[:, 0, t * DM:(t + 1) * DM], hid[:, a, t * P:(t + 1) * P],
                                      w2[:, a, :], a == 0, False)
                        if b:
                            last = mm(po[:, 0, t * DM:(t + 1) * DM], one[0:1, 0:1].broadcast_to([1, P]), b2[:],
                                      False, True)
                        if t and b:
                            last.then_inc(s_f2[p], 1)


def kernel(**inputs):
    import concourse.bacc as bacc
    from concourse.bass_utils import run_bass_kernel_spmd

    get = {name: np.asarray(a) for name, a in inputs.items()}
    x = get["L0_attn_hidden_states"]
    arrays = {
        "x": x,
        "xT": x.reshape(BATCH * SEQ, DM).T,
        "winT": get["L0_attn_in_proj_w"].T,
        "conv_w": get["L0_attn_conv_w"],
        "conv_b": get["L0_attn_conv_b"],
        "xpT": get["L0_attn_x_proj_w"].T,
        "dtT": get["L0_attn_dt_proj_w"].T,
        "dt_b": get["L0_attn_dt_proj_b"],
        "A_log": get["L0_attn_A_log"],
        "D": get["L0_attn_D"],
        "woT": get["L0_attn_out_proj_w"].T,
        "w1": get["L0_ffn_w1"],
        "b1": get["L0_ffn_b1"],
        "w2": get["L0_ffn_w2"],
        "b2": get["L0_ffn_b2"],
    }
    for name in ("conv_b", "D", "b1"):
        arrays[name] = arrays[name].reshape(-1, P).T
    arrays = {f"in_{name}": np.ascontiguousarray(a) for name, a in arrays.items()}
    nc = bacc.Bacc("TRN2", target_bir_lowering=False, num_devices=1)
    args = [nc.dram_tensor(name, a.shape, mybir.dt.from_np(a.dtype), kind="ExternalInput").ap()
            for name, a in arrays.items()]
    out = nc.dram_tensor("out", x.shape, F32, kind="ExternalOutput").ap()
    build(nc, *args, out)
    r = run_bass_kernel_spmd(nc, [arrays], core_ids=[0])
    return r.results[0]["out"]
```
